# Optimizing a Trainium2 kernel written in Bass

```python
import numpy as np
import jax
import jax.numpy as jnp

def _softmax(x, axis=-1):
    return jax.nn.softmax(x, axis=axis)

def _gelu(x):
    return jax.nn.gelu(x, approximate=True)

def _silu(x):
    return jax.nn.silu(x)

def _sigmoid(x):
    return jax.nn.sigmoid(x)

def _layernorm(x, axis=-1, eps=1e-05):
    m = jnp.mean(x, axis=axis, keepdims=True)
    v = jnp.var(x, axis=axis, keepdims=True)
    return (x - m) / jnp.sqrt(v + eps)

def _scatter_add(tgt, idx, src, axis=0):
    return tgt.at[idx].add(src)

def _segment_sum(src, seg, n):
    return jax.ops.segment_sum(src, seg, n)
kernel_name = 'mk_seq_preln_d1_jaxref_r4_d8db09'

def setup_inputs(seed: int=0):
    np.random.seed(seed)
    _w = jnp.asarray

    def _L0_attn_setup():
        import jax, jax.numpy as jnp
        import numpy as np
        B, T, D_MODEL = (4, 1024, 512)
        D_LATENT = 128
        D_COMP = 64
        THETA = 10000.0
        LN_EPS = 1e-05

        def _rope_tables(seq_len: int, dim: int):
            inv_freq = 1.0 / THETA ** (jnp.arange(0, dim, 2, dtype=jnp.float32) / dim)
            freqs = jnp.arange(seq_len, dtype=jnp.float32)[:, None] * inv_freq[None, :]
            cos = jnp.concatenate([jnp.cos(freqs), jnp.cos(freqs)], axis=-1)
            sin = jnp.concatenate([jnp.sin(freqs), jnp.sin(freqs)], axis=-1)
            return (cos, sin)

        def _rotate_half(x):
            x1, x2 = jnp.split(x, 2, axis=-1)
            return jnp.concatenate([-x2, x1], axis=-1)
        key = jax.random.key(seed)
        ks = jax.random.split(key, 8)
        s = 0.02
        return {'x': jax.random.normal(ks[0], (B, T, D_MODEL), dtype=jnp.float32), 'W_to_kv': jax.random.normal(ks[1], (D_LATENT, D_MODEL), dtype=jnp.float32) * s, 'W_compress': jax.random.normal(ks[2], (D_COMP, D_LATENT), dtype=jnp.float32) * s, 'ln_gamma': jnp.ones((D_COMP,), dtype=jnp.float32), 'ln_beta': jnp.zeros((D_COMP,), dtype=jnp.float32), 'W_q_comp': jax.random.normal(ks[3], (D_COMP, D_COMP), dtype=jnp.float32) * s, 'W_kv_comp': jax.random.normal(ks[4], (2 * D_COMP, D_COMP), dtype=jnp.float32) * s, 'W_comp2lat': jax.random.normal(ks[5], (D_LATENT, D_COMP), dtype=jnp.float32) * s, 'W_out_res': jnp.zeros((D_MODEL, D_LATENT), dtype=jnp.float32), 'b_out_res': jnp.zeros((D_MODEL,), dtype=jnp.float32)}
    _L0_attn_in = _L0_attn_setup()

    def _L0_ffn_setup():
        import jax, jax.numpy as jnp
        import numpy as np
        B, S, D, H = (4, 512, 512, 2048)

        def fwht(x):
            orig_shape = x.shape
            n = orig_shape[-1]
            x = x.reshape(-1, n)
            h = 1
            while h < n:
                xb = x.reshape(-1, n // (2 * h), 2, h)
                a = xb[:, :, 0, :]
                b = xb[:, :, 1, :]
                x = jnp.stack([a + b, a - b], axis=2).reshape(-1, n)
                h *= 2
            scale = jnp.asarray(1.0 / np.sqrt(n), dtype=x.dtype)
            return (x * scale).reshape(orig_shape)
        key = jax.random.key(seed)
        kx, k1, k2, k3 = jax.random.split(key, 4)
        x = jax.random.normal(kx, (B, S, D), dtype=jnp.float32)
        W1 = jax.random.normal(k1, (H, D), dtype=jnp.float32) * (1.0 / np.sqrt(D))
        W2 = jax.random.normal(k2, (D, H), dtype=jnp.float32) * (1.0 / np.sqrt(H))
        W3 = jax.random.normal(k3, (H, D), dtype=jnp.float32) * (1.0 / np.sqrt(D))
        return {'x': x, 'W1': W1, 'W2': W2, 'W3': W3}
    _L0_ffn_in = _L0_ffn_setup()
    _d = {'L0_attn_x': _L0_attn_in['x'], 'L0_attn_W_to_kv': _L0_attn_in['W_to_kv'], 'L0_attn_W_compress': _L0_attn_in['W_compress'], 'L0_attn_ln_gamma': _L0_attn_in['ln_gamma'], 'L0_attn_ln_beta': _L0_attn_in['ln_beta'], 'L0_attn_W_q_comp': _L0_attn_in['W_q_comp'], 'L0_attn_W_kv_comp': _L0_attn_in['W_kv_comp'], 'L0_attn_W_comp2lat': _L0_attn_in['W_comp2lat'], 'L0_attn_W_out_res': _L0_attn_in['W_out_res'], 'L0_attn_b_out_res': _L0_attn_in['b_out_res'], 'L0_ffn_W1': _L0_ffn_in['W1'], 'L0_ffn_W2': _L0_ffn_in['W2'], 'L0_ffn_W3': _L0_ffn_in['W3']}
    _x0 = _d['L0_attn_x']
    _d['L0_attn_x'] = jax.random.normal(jax.random.fold_in(jax.random.key(seed), 1), (8, 1024, 512), dtype=_x0.dtype)
    del _x0
    return _d

def reference(L0_attn_x, L0_attn_W_to_kv, L0_attn_W_compress, L0_attn_ln_gamma, L0_attn_ln_beta, L0_attn_W_q_comp, L0_attn_W_kv_comp, L0_attn_W_comp2lat, L0_attn_W_out_res, L0_attn_b_out_res, L0_ffn_W1, L0_ffn_W2, L0_ffn_W3):

    def _L0_attn_ref(x, W_to_kv, W_compress, ln_gamma, ln_beta, W_q_comp, W_kv_comp, W_comp2lat, W_out_res, b_out_res):
        import jax, jax.numpy as jnp
        import numpy as np
        B, T, D_MODEL = (4, 1024, 512)
        D_LATENT = 128
        D_COMP = 64
        THETA = 10000.0
        LN_EPS = 1e-05

        def _rope_tables(seq_len: int, dim: int):
            inv_freq = 1.0 / THETA ** (jnp.arange(0, dim, 2, dtype=jnp.float32) / dim)
            freqs = jnp.arange(seq_len, dtype=jnp.float32)[:, None] * inv_freq[None, :]
            cos = jnp.concatenate([jnp.cos(freqs), jnp.cos(freqs)], axis=-1)
            sin = jnp.concatenate([jnp.sin(freqs), jnp.sin(freqs)], axis=-1)
            return (cos, sin)

        def _rotate_half(x):
            x1, x2 = jnp.split(x, 2, axis=-1)
            return jnp.concatenate([-x2, x1], axis=-1)
        Bx, Tx, _ = x.shape
        dc = W_compress.shape[0]
        kv_latent = x @ W_to_kv.T
        c = kv_latent @ W_compress.T
        mu = jnp.mean(c, axis=-1, keepdims=True)
        var = jnp.mean((c - mu) ** 2, axis=-1, keepdims=True)
        ch = (c - mu) * jax.lax.rsqrt(var + LN_EPS) * ln_gamma + ln_beta
        q = ch @ W_q_comp.T
        kv = ch @ W_kv_comp.T
        k, v = jnp.split(kv, 2, axis=-1)
        cos, sin = _rope_tables(Tx, dc)
        q = q * cos + _rotate_half(q) * sin
        k = k * cos + _rotate_half(k) * sin
        scale = 1.0 / jnp.sqrt(jnp.float32(dc))
        scores = jnp.einsum('btd,bsd->bts', q, k) * scale
        causal = jnp.tril(jnp.ones((Tx, Tx), dtype=bool))
        scores = jnp.where(causal[None], scores, jnp.float32(-1e+30))
        attn = jax.nn.softmax(scores, axis=-1)
        o = jnp.einsum('bts,bsd->btd', attn, v)
        z = o @ W_comp2lat.T
        out = z @ W_to_kv + z @ W_out_res.T + b_out_res
        return out

    def _L0_ffn_ref(x, W1, W2, W3):
        import jax, jax.numpy as jnp
        import numpy as np
        B, S, D, H = (4, 512, 512, 2048)

        def fwht(x):
            orig_shape = x.shape
            n = orig_shape[-1]
            x = x.reshape(-1, n)
            h = 1
            while h < n:
                xb = x.reshape(-1, n // (2 * h), 2, h)
                a = xb[:, :, 0, :]
                b = xb[:, :, 1, :]
                x = jnp.stack([a + b, a - b], axis=2).reshape(-1, n)
                h *= 2
            scale = jnp.asarray(1.0 / np.sqrt(n), dtype=x.dtype)
            return (x * scale).reshape(orig_shape)
        up_gate = jnp.einsum('bsd,hd->bsh', x, W1)
        up_lin = jnp.einsum('bsd,hd->bsh', x, W3)
        hidden = jax.nn.silu(up_gate) * up_lin
        hidden = fwht(hidden)
        out = jnp.einsum('bsh,dh->bsd', hidden, W2)
        return out
    x = L0_attn_x
    x = x + _L0_attn_ref(_layernorm(x, axis=-1), L0_attn_W_to_kv, L0_attn_W_compress, L0_attn_ln_gamma, L0_attn_ln_beta, L0_attn_W_q_comp, L0_attn_W_kv_comp, L0_attn_W_comp2lat, L0_attn_W_out_res, L0_attn_b_out_res)
    x = x + _L0_ffn_ref(_layernorm(x, axis=-1), L0_ffn_W1, L0_ffn_W2, L0_ffn_W3)
    return x

_drawn_inputs = setup_inputs


def setup_inputs(seed=0):
    import zlib

    import numpy as np

    out = dict(_drawn_inputs(seed))
    spreads = {'L0_attn_ln_gamma': (1.0, 0.6),
     'L0_attn_ln_beta': (0.0, 0.8),
     'L0_attn_W_out_res': (0.0, 0.8),
     'L0_attn_b_out_res': (0.0, 0.8)}
    factors = {'L0_attn_W_to_kv': 8.0,
     'L0_attn_W_compress': 8.0,
     'L0_attn_W_q_comp': 8.0,
     'L0_attn_W_kv_comp': 8.0,
     'L0_attn_W_comp2lat': 8.0}
    for name, (base, spread) in spreads.items():
        noise = np.random.default_rng([zlib.crc32(name.encode()), seed]).standard_normal(out[name].shape)
        drawn = base * np.exp(spread * noise) if base else spread * noise
        out[name] = jnp.asarray(drawn.astype(out[name].dtype))
    for name, factor in factors.items():
        out[name] = (out[name] * factor).astype(out[name].dtype)
    return out
```

```python
from contextlib import ExitStack

import numpy as np
import concourse.bass as bass
from concourse import mybir

F32 = mybir.dt.float32
F32R = mybir.dt.float32r
F16 = mybir.dt.float16
BF16 = mybir.dt.bfloat16
I32 = mybir.dt.int32
ALU = mybir.AluOpType
ACT = mybir.ActivationFunctionType
AX = mybir.AxisListType

NC = 16
NH = 16
EPS = 1e-5
WTK, WCT, WQ, WK, WV, WCL, WOR, GB, BIAS, NSM = 0, 512, 576, 640, 704, 832, 896, 1408, 1410, 1922
HAD, IDN, IDD, MSK, NCST = 0, 128, 256, 320, 576


class Program:

    ENG = ("tensor", "vector", "scalar", "gpsimd", "sync")

    def __init__(self, nc, ctx):
        self.nc, self.ctx = nc, ctx
        self.queue = {e: [] for e in self.ENG}
        self.sems, self.count = {}, {}

    def sem(self, name):
        if name not in self.sems:
            self.sems[name] = self.ctx.enter_context(self.nc.semaphore(name))
            self.count[name] = 0
        return self.sems[name]

    def put(self, eng, fn, waits, sem, by=1):
        self.sem(sem)
        self.count[sem] += by
        self.queue[eng].append((fn, [w for w in waits if w is not None], sem, by))
        return sem, self.count[sem]

    def play(self, eng_name, eng):
        seen = {}
        for fn, waits, sem, by in self.queue[eng_name]:
            for s, v in waits:
                if seen.get(s, 0) < v:
                    eng.wait_ge(self.sems[s], v)
                    seen[s] = v
            fn(eng).then_inc(self.sems[sem], by)


def build_kernel(nc, x, xT, w13, w2, small, cst, tab, out):
    with ExitStack() as ctx:
        P = Program(nc, ctx)

        def sb(name, shape, dt):
            return ctx.enter_context(nc.sbuf_tensor(name, shape, dt))

        WA = sb("WA", [128, NH * 2048], F16)
        W2 = sb("W2s", [128, NH, 2, 512], F16)
        ring = sb("ring", [128, 8, 512], F32)
        xnT = [sb(f"xnT{i}", [128, 2, 4, 512], F16) for i in range(2)]
        sil = sb("sil", [128, 512], F32)
        hd = sb("hd", [128, 512], F32)
        hT = sb("hT", [128, 2, 2, 512], F16)
        cosT = sb("cosT", [128, 1024], F32)
        sinT = sb("sinT", [128, 1024], F32)
        Q = sb("Q", [128, 512], F32R)
        Kh = sb("Kh", [128, 1024], F32R)
        Kl = sb("Kl", [128, 1024], F32R)
        V = sb("V", [128, 8, 128], F16)
        xraw = sb("xraw", [128, 2, 512], F32)
        xh = sb("xh", [128, 512], F32R)
        xl = sb("xl", [128, 512], F32R)
        VT = sb("VT", [128, 512], F32R)
        xs = sb("xs", [128, 512], F32)
        xnp = sb("xnp", [128, 2, 512], F16)
        PB = sb("PB", [128, 1024], F32)
        Ph = sb("Ph", [128, 1024], F16)
        Pl = sb("Pl", [128, 1024], F16)
        PT = sb("PT", [128, 2, 1024], F16)
        oh = sb("oh", [128, 128], F32R)
        ol = sb("ol", [128, 128], F32R)
        Mh = sb("Mh", [128, 512], F32R)
        Ml = sb("Ml", [128, 512], F32R)
        bb = sb("bb", [128, 512], F32)
        Wc = sb("Wc", [128, 4, 128], F32R)
        Wph = sb("Wph", [128, 4, 128], F32R)
        Wpl = sb("Wpl", [128, 4, 128], F32R)
        cs = sb("cst_s", [128, NCST], F32)
        id16 = sb("id16", [128, 128], F16)
        idbf = sb("idbf", [128, 128], BF16)
        one1 = sb("one1", [128, 1], BF16)
        srow = sb("srow", [128, 2, 2048], BF16)
        st = sb("st", [128, 160], F32)
        sti = sb("sti", [128, 160], I32)
        afs = sb("afs", [128, 80], F32)
        pbias = sb("pbias", [128, 4], F32)
        sbf = sb("sbf", [128, 32], BF16)

        xTc = xs
        wsm = xnT[1][:, :, :, :].rearrange("p a b c -> p (a b c)").bitcast(F32)
        Fw = WA[:, :].bitcast(F32)
        F0, F1 = Fw[:, 0:8192], Fw[:, 8192:16384]

        XY = ctx.enter_context(nc.psum_tensor("XY", [128, 1024], F32))
        PG = ctx.enter_context(nc.psum_tensor("PG", [128, 512], F32))
        PU = ctx.enter_context(nc.psum_tensor("PU", [128, 512], F32))
        PD = ctx.enter_context(nc.psum_tensor("PD", [128, 4, 512], F32))
        X, Y = XY[:, 0:512], XY[:, 512:1024]
        X16, Y16 = X.bitcast(F16), Y.bitcast(F16)

        had, idn = cs[:, HAD:HAD + 128], cs[:, IDN:IDN + 128]
        idd, msk = cs[:, IDD:IDD + 64], cs[:, MSK:MSK + 256]
        gam, bet = wsm[:, GB:GB + 1], wsm[:, GB + 1:GB + 2]

        def mm(parts, waits, sem="pe"):
            def go(e):
                for o, l, r, a, z in parts:
                    last = e.matmul(o, l, r, start=a, stop=z)
                return last
            return P.put("tensor", go, waits, sem)

        def tr(parts, ident, waits, sem="pe"):
            def go(e):
                for o, i in parts:
                    last = e.transpose(o, i, ident)
                return last
            return P.put("tensor", go, waits, sem)

        def act(o, i, func, waits, sem="act", **kw):
            return P.put("scalar", lambda e: e.activation(o, i, func, **kw), waits, sem)

        def tt(o, a, b, op, waits, sem="dve", eng="vector"):
            return P.put(eng, lambda e: e.tensor_tensor(o, a, b, op), waits, sem)

        def ts(o, a, s1, s2, op0, op1, waits, sem="dve"):
            if op1 is None:
                return P.put("vector", lambda e: e.tensor_scalar(o, a, s1, None, op0), waits, sem)
            return P.put("vector", lambda e: e.tensor_scalar(o, a, s1, s2, op0, op1), waits, sem)

        def stt(o, a, s, b, op0, op1, waits, sem="dve"):
            return P.put("vector", lambda e: e.scalar_tensor_tensor(o, a, s, b, op0, op1), waits, sem)

        def red(o, i, op, waits, sem="dve", **kw):
            return P.put("vector", lambda e: e.tensor_reduce(o, i, AX.X, op, **kw), waits, sem)

        def dma(o, i, waits, sem):
            return P.put("sync", lambda e: e.dma_start(o, i), waits, sem, 16)

        def rsqrt(v, y, t, ti, waits):
            k = ts(ti, v.bitcast(I32), 1, None, ALU.logical_shift_right, None, waits)
            k = ts(y.bitcast(I32), ti, -1.0, 1597463007.0, ALU.mult, ALU.add, [k])
            for _ in range(4):
                k = tt(t, y, y, ALU.mult, [k])
                k = tt(t, t, v, ALU.mult, [k])
                k = ts(t, t, -0.5, 1.5, ALU.mult, ALU.add, [k])
                k = tt(y, y, t, ALU.mult, [k])
            return k

        T = {}

        k_sm = dma(wsm[:, 0:NSM], small, [], "d_small")
        k_cst = dma(cs[:, :], cst, [], "d_cst")
        k_tab = [dma(t[:, :], tab[i], [], f"d_tab{i}") for i, t in enumerate((cosT, sinT))]

        def load_x(n):
            for t in range(4):
                r = (n % 2) * 4 + t
                w = [T["store", n - 2, t]] if n >= 2 else ([T["wp", NH - 1]] if n == 1 else [])
                T["x", n, t] = dma(ring[:, r, :], x[(n * 4 + t) * 128:(n * 4 + t + 1) * 128, :], w, f"d_x{r}")

        def load_xT(n, k):
            w = [T["xl", n, k - 2]] if k >= 2 else ([T["xl", n - 1, k + 2]] if n else [])
            T["xT", n, k] = dma(xraw[:, k % 2, :], xT[n, :, k, :], w, f"d_xT{k % 2}")

        load_xT(0, 0)
        load_xT(0, 1)
        load_x(0)
        for q in range(4):
            T["w2", q] = dma(F0[:, q * 2048:(q + 1) * 2048], w2[:, q * 2048:(q + 1) * 2048], [], f"d_w2{q}")

        k_i16 = act(id16[:, :], idn, ACT.Copy, [k_cst])
        k_ibf = act(idbf[:, :], idn, ACT.Copy, [k_cst])
        k_one = P.put("gpsimd", lambda e: e.memset(one1[:, :], 1.0), [], "pool")

        def small_weights():
            m1, m2 = st[:, 0:1], st[:, 1:2]
            k1 = red(m1, wsm[:, WTK:WTK + 512], ALU.add, [k_sm])
            k1 = ts(m1, m1, 1.0 / 512, None, ALU.mult, None, [k1])
            kt = ts(PB[:, 0:512], wsm[:, WTK:WTK + 512], m1, None, ALU.subtract, None, [k1])
            k2 = red(m2, wsm[:, WCT:WCT + 64], ALU.add, [k_sm])
            k2 = ts(m2, m2, 1.0 / 64, None, ALU.mult, None, [k2])
            kc = ts(PB[:, 512:576], wsm[:, WCT:WCT + 64], m2, None, ALU.subtract, None, [k2])
            km = mm([(X[:, k * 64:(k + 1) * 64], PB[:, k * 128:(k + 1) * 128], PB[:, 512:576], True, True)
                     for k in range(4)], [kt, kc])
            xv = X[:, 0:256].rearrange("p (k c) -> p k c", k=4)
            kh = P.put("vector", lambda e: e.tensor_copy(Wc[:, :, 0:64], xv), [km], "dve")
            T["Wc"] = tt(Wc[:, :, 64:128], xv, Wc[:, :, 0:64].bitcast(F32), ALU.subtract, [kh])
            wf = PB[:, 0:512].rearrange("p (i c) -> p i c", i=4)
            ks = [km]
            for i, base in ((0, WQ), (2, WK)):
                for h in range(2):
                    src = wsm[:, base:base + 64]
                    ks.append(ts(wf[:, i, h * 64:h * 64 + 64], src, 1.0, None, ALU.mult, None, [k_sm, km]))
                    ks.append(ts(wf[:, i + 1, h * 64:h * 64 + 32], src[:, 32:64], -1.0, None, ALU.mult, None, [km]))
                    ks.append(ts(wf[:, i + 1, h * 64 + 32:h * 64 + 64], src[:, 0:32], 1.0, None, ALU.mult, None, [km]))
            kb = mm([(Y[:, i:i + 1], wf[0:64, i, :], bet[0:64, :], True, True) for i in range(4)], [ks[-1]])
            T["pbias"] = P.put("vector", lambda e: e.tensor_copy(pbias[:, :], Y[:, 0:4]), [kb], "dve")
            wg = xs[:, :].rearrange("p (i c) -> p i c", i=4)
            kg = ts(wg, wf, gam, None, ALU.mult, None, [ks[-1]])
            kh = P.put("vector", lambda e: e.tensor_copy(Wph[:, :, :], wg), [kg], "dve")
            T["Wp"] = tt(Wpl[:, :, :], wg, Wph[:, :, :].bitcast(F32), ALU.subtract, [kh])
            ka = tt(PB[:, 512:1024], wsm[:, WTK:WTK + 512], wsm[:, WOR:WOR + 512], ALU.add, [k_sm, km])
            k1 = mm([(Y[0:64, :], wsm[:, WCL:WCL + 64], PB[:, 512:1024], True, True)], [ka, T["pbias"]])
            k1 = P.put("vector", lambda e: e.tensor_copy(PB[0:64, 0:512], Y[0:64, :]), [k1, T["Wp"], kb], "dve")
            k1 = mm([(X, wsm[0:64, WV:WV + 128], PB[0:64, 0:512], True, True)], [k1, T["Wc"]])
            kM = P.put("vector", lambda e: e.tensor_copy(PB[:, 512:1024], X), [k1], "dve")
            kb = mm([(Y, bet[0:64, :].broadcast_to([64, 128]), PB[0:64, 512:1024], True, True)], [kM, k1])
            T["bb"] = tt(bb[:, :], Y, wsm[:, BIAS:BIAS + 512], ALU.add, [kb])
            kg = ts(PB[:, 0:512], PB[:, 512:1024], gam, None, ALU.mult, None, [kM])
            kh = P.put("vector", lambda e: e.tensor_copy(Mh[:, :], PB[:, 0:512]), [kg], "dve")
            T["M"] = tt(Ml[:, :], PB[:, 0:512], Mh[:, :].bitcast(F32), ALU.subtract, [kh])

        def attention(n):
            c, first = n % 2, n == 0
            pos = c * 512
            steps = []

            def stats():
                load_x(n)

            def xstats():
                for t in range(4):
                    r = (n % 2) * 4 + t
                    k = P.put("vector", lambda e, t=t, r=r: e.bn_stats(st[:, 8 + 6 * t:14 + 6 * t], ring[:, r, :]),
                              [T["x", n, t]], "dve")
                    T["xs1", n, t] = k
                for t in range(4):
                    r = (n % 2) * 4 + t
                    k = P.put("vector", lambda e, t=t: e.bn_aggr(st[:, 32 + 2 * t:34 + 2 * t], st[:, 8 + 6 * t:14 + 6 * t]),
                              [T["xs1", n, t]], "dve")
                    T["xb", n, t] = tt(ring[:, r, :], ring[:, r, :], bb[:, :], ALU.add,
                                       [T["xs1", n, t], T["bb"]], "pool", "gpsimd")
                T["xst", n] = k

            def conv(k):
                def go():
                    w = [T["xT", n, k], T["cp", n, k - 1] if k else T.get(("cp", n - 1, 3))]
                    T["xh", n, k] = act(xh[:, :], xraw[:, k % 2, :], ACT.Copy, w)
                    T["xl", n, k] = tt(xl[:, :], xraw[:, k % 2, :], xh[:, :].bitcast(F32), ALU.subtract,
                                       [T["xh", n, k], w[1]])
                    if k < 2:
                        load_xT(n, k + 2)
                return go

            def cproj(k):
                def go():
                    T["cp", n, k] = mm([(X, Wc[:, k, :], xh[:, :], k == 0, False),
                                        (X, Wc[:, k, :], xl[:, :], False, k == 3)],
                                       [T["xl", n, k], T["Wc"], T.get("Xfree")])
                return go

            def latent():
                T["cT"] = act(xTc[:, :], X, ACT.Copy, [T["cp", n, 3], T.get("xsfree"), T.get("Wp")])
                T["Xfree"] = T["cT"]

            def latent2():
                T["ct"] = mm([(Y[:, t * 64:t * 64 + 64], xTc[:, t * 128:(t + 1) * 128], idd, True, True)
                              for t in range(4)], [T["cT"], T.get("Yfree"), k_cst])

            def norm1():
                c0, c1 = PB[:, 0:256], PB[:, 256:512]
                c3 = c0.rearrange("p (t c) -> p t c", t=4)
                k0 = P.put("vector", lambda e: e.tensor_copy(c0, Y[:, 0:256]), [T["ct"], T.get("PBfree"), T.get("M")], "dve")
                T["Yfree"] = k0
                k = tt(c1, c0, c0, ALU.mult, [k0])
                k = red(st[:, 40:44], c1.rearrange("p (t c) -> p t c", t=4), ALU.add, [k])
                var = st[:, 32:40].rearrange("p (t c) -> p t c", t=4)[:, :, 1]
                k2 = ts(st[:, 44:48], var, EPS, EPS * EPS, ALU.mult, ALU.add, [T["xst", n]])
                k = stt(st[:, 48:52], st[:, 40:44], 1.0 / 64, st[:, 44:48], ALU.mult, ALU.add, [k, k2])
                k = rsqrt(st[:, 48:52], st[:, 52:56], st[:, 56:60], sti[:, 0:4], [k])
                k = ts(st[:, 52:56], st[:, 52:56], 256.0, None, ALU.mult, None, [k])
                cn = c1.rearrange("p (t c) -> p t c", t=4)
                k = tt(cn, c3, st[:, 52:56].unsqueeze(2).broadcast_to([128, 4, 64]), ALU.mult, [k])
                vh, vl = V[:, 4 * c:4 * c + 4, 0:64], V[:, 4 * c:4 * c + 4, 64:128]
                k = P.put("vector", lambda e: e.tensor_copy(vh, cn), [k, T.get("PVlast")], "dve")
                T["V", n] = tt(vl, cn, vh, ALU.subtract, [k])

            def vT():
                k = tr([(X16[:, t * 128:(t + 1) * 128], V[:, 4 * c + t, :]) for t in range(4)], id16[:, :],
                       [T["V", n], T["Xfree"], k_i16])
                T["VT"] = act(VT[:, :], X16[:, 0:512], ACT.Copy, [k, T.get("VTfree")], scale=1.0 / 256)
                T["Xfree"] = T["VT"]

            def proj(i):
                def go():
                    T["pj", i] = mm([(X, Wph[:, i, :], VT[:, :], True, False), (X, Wpl[:, i, :], VT[:, :], False, True),
                                     (Y, Wph[:, i + 1, :], VT[:, :], True, False), (Y, Wpl[:, i + 1, :], VT[:, :], False, True)],
                                    [T["VT"], T["Xfree"], T["Yfree"], T["Wp"]])
                    T["VTfree"] = T["pj", i]
                    a, b = PB[:, 0:512], PB[:, 512:1024]
                    ka = stt(a, X, pbias[:, i:i + 1], cosT[:, pos:pos + 512], ALU.add, ALU.mult,
                             [T["pj", i], T["V", n], T.get("rope"), T["pbias"], k_tab[0]])
                    T["Xfree"] = ka
                    kb = stt(b, Y, pbias[:, i + 1:i + 2], sinT[:, pos:pos + 512], ALU.add, ALU.mult,
                             [T["pj", i], T.get("rope"), T.get("PBfree"), k_tab[1]])
                    T["Yfree"] = kb
                    k = tt(a, a, b, ALU.add, [ka, kb])
                    if i == 0:
                        kq = act(Q[:, :], a, ACT.Copy, [k, T.get("Qfree")])
                        T["Q"] = tt(Q[64:128, :], a[64:128, :], Q[64:128, :].bitcast(F32), ALU.subtract, [kq])
                    else:
                        kk = act(Kh[:, pos:pos + 512], a, ACT.Copy, [k, T.get("Qfree")])
                        T["K"] = tt(Kl[:, pos:pos + 512], a, Kh[:, pos:pos + 512].bitcast(F32), ALU.subtract, [kk])
                    T["rope"] = T["Q"] if i == 0 else T["K"]
                return go

            def tile(ti):
                t, ns = ti % 4, ti + 1
                W = max(256, ns * 128)
                r = (n % 2) * 4 + t
                q = Q[:, t * 128:(t + 1) * 128]
                c_ = 64 + 8 * (ti % 2)
                nmax, rsum, rinv = st[:, c_:c_ + 1], st[:, c_ + 1:c_ + 2], st[:, c_ + 2:c_ + 3]

                def scores():
                    parts = []
                    for a in range(0, W, 512):
                        z = min(W, a + 512)
                        if z - a < 256:
                            z = a + 256
                        parts += [(XY[:, a:z], q, Kh[:, a:z], True, False), (XY[:, a:z], q, Kl[:, a:z], False, True)]
                    w = [T["Q"], T["K"], T["Xfree"]] + ([T["Yfree"]] if W > 512 else [])
                    k = mm(parts, w)
                    T["Qfree"] = k
                    d = (ns - 1) * 128
                    k = tt(XY[:, d:d + 128], XY[:, d:d + 128], msk[:, 0:128], ALU.add, [k])
                    k = red(rsum, XY[:, 0:ns * 128], ALU.max, [k, T.get(("rinv", ti % 2))])
                    T["nmax"] = ts(nmax, rsum, -0.125, None, ALU.mult, None, [k, T.get(("exp", ti % 2))])

                def exps():
                    w = ns * 128
                    k = P.put("scalar", lambda e: e.activation(PB[:, 0:w], XY[:, 0:w], ACT.Exp, bias=nmax, scale=0.125,
                                                               accum_out=rsum), [T["nmax"], T.get("Pl"), T["rope"]], "act")
                    T["exp", ti % 2] = k
                    T["Xfree"] = k
                    if w > 512:
                        T["Yfree"] = k
                    T["Ph"] = act(Ph[:, 0:w], PB[:, 0:w], ACT.Copy, [k, T.get("Tlast")], scale=4096.0)

                def low():
                    w = ns * 128
                    T["Pl"] = stt(Pl[:, 0:w], PB[:, 0:w], 4096.0, Ph[:, 0:w], ALU.mult, ALU.subtract, [T["Ph"], T.get("Tlast")])
                    T["PBfree"] = T["Pl"]
                    k = ts(rinv, rsum, float(2 ** 20), None, ALU.mult, None, [T["exp", ti % 2], T.get(("x2", ti % 2))])
                    T["rinv", ti % 2] = P.put("vector", lambda e: e.reciprocal(rinv, rinv), [k], "dve")

                def trans(g):
                    s0, s1 = 4 * g, min(ns, 4 * g + 4)
                    m = s1 - s0
                    k = tr([(Y16[:, (h * m + s) * 128:(h * m + s + 1) * 128], (Ph, Pl)[h][:, (s0 + s) * 128:(s0 + s + 1) * 128])
                            for h in range(2) for s in range(m)], id16[:, :], [T["Pl"], T["Yfree"]])
                    T["Tlast"] = k
                    k = act(PT[:, g, 0:2 * m * 128], Y16[:, 0:2 * m * 128], ACT.Copy, [k, T.get(("PVg", g))])
                    T["Yfree"] = T["PT", g] = k

                def pv(g):
                    s0, s1 = 4 * g, min(ns, 4 * g + 4)
                    m = s1 - s0
                    parts = [(X[:, 0:128], V[:, s0 + s, :], PT[:, g, (h * m + s) * 128:(h * m + s + 1) * 128],
                              s0 + s == 0 and h == 0, s0 + s == ns - 1 and h == 1)
                             for s in range(m) for h in range(2)]
                    k = mm(parts, [T["PT", g], T["Xfree"]])
                    T["PVg", g] = T["PVlast"] = k
                    if s1 == ns:
                        k = P.put("vector", lambda e: e.tensor_copy(oh[:, :], X[:, 0:128]), [k, T.get("opm")], "dve")
                        T["o"] = T["Xfree"] = tt(ol[:, :], X[:, 0:128], oh[:, :].bitcast(F32), ALU.subtract, [k])

                def outp():
                    T["opm"] = k = mm([(Y, oh[:, :], Mh[:, :], True, False), (Y, oh[:, :], Ml[:, :], False, False),
                                       (Y, ol[:, :], Mh[:, :], False, True)], [T["o"], T["Yfree"], T["M"]])
                    xt = ring[:, r, :]
                    k = stt(xt, Y, rinv, xt, ALU.mult, ALU.add, [k, T["rinv", ti % 2], T["xb", n, t]])
                    T["x2", ti % 2] = T["Yfree"] = k
                    k = P.put("vector", lambda e: e.bn_stats(st[:, 80:86], xt), [k], "dve")
                    k = P.put("vector", lambda e: e.bn_aggr(st[:, 86:88], st[:, 80:86]), [k], "dve")
                    k = ts(st[:, 88:89], st[:, 87:88], EPS, None, ALU.add, None, [k])
                    k = rsqrt(st[:, 88:89], st[:, 89:90], st[:, 90:91], sti[:, 8:9], [k])
                    k = ts(st[:, 89:90], st[:, 89:90], 1024.0, None, ALU.mult, None, [k])
                    k = ts(xs[:, :], xt, st[:, 86:87], st[:, 89:90], ALU.subtract, ALU.mult, [k, T.get("xh16"), T["ct"]])
                    T["xh16"] = act(xnp[:, 0, :], xs[:, :], ACT.Copy, [k, T.get("XT")])
                    T["xn16"] = tt(xnp[:, 1, :], xs[:, :], xnp[:, 0, :], ALU.subtract, [T["xh16"], T.get("XT")])
                    T["xsfree"] = T["xn16"]

                def xtr():
                    T["XT"] = k = tr([(X16[:, (h * 4 + j) * 128:(h * 4 + j + 1) * 128], xnp[:, h, j * 128:(j + 1) * 128])
                                      for h in range(2) for j in range(4)], id16[:, :], [T["xn16"], T["Xfree"]])
                    k = act(xnT[n % 2][:, :, :, t * 128:(t + 1) * 128], X16.rearrange("p (h j c) -> p h j c", h=2, j=4),
                            ACT.Copy, [k, T.get(("Uend", n - 2))] + ([T["bb"], T["M"], T["pbias"]] if n == 1 else []))
                    T["Xfree"] = T["xn", n, t] = k

                out_ = [scores, exps, low, lambda: trans(0)]
                if ns > 4:
                    out_ += [lambda: (pv(0), trans(1)), lambda: pv(1)]
                else:
                    out_ += [lambda: pv(0)]
                return out_ + [outp, xtr]

            if n:
                steps.append(lambda: (stats(), load_xT(n, 0), load_xT(n, 1)))
            steps.append(xstats)
            steps.append(conv(0))
            for k in range(4):
                steps.append(lambda k=k: (cproj(k)(), conv(k + 1)() if k < 3 else None))
            steps += [latent, latent2, norm1, vT, proj(0), proj(2)]
            for ti in range(4 * c, 4 * c + 4):
                steps += tile(ti)
            return steps

        def butterfly(s, q):
            h = 1 << s
            src, dst = (F0, F1) if s % 2 == 0 else (F1, F0)
            a = src.rearrange("p (g two h n) -> p g two h n", two=2, h=h, n=512)
            b = dst.rearrange("p (g two h n) -> p g two h n", two=2, h=h, n=512)
            pairs = [(g, i) for g in range(8 // h) for i in range(h)]
            w = [T["w2", i] for i in range(4)] if s == 0 else [T["bf", s - 1]]
            for g, i in pairs[2 * q:2 * q + 2]:
                u, v = a[:, g, 0, i, :], a[:, g, 1, i, :]
                tt(b[:, g, 0, i, :], u, v, ALU.add, w)
                k = tt(b[:, g, 1, i, :], u, v, ALU.subtract, w)
            if q == 3:
                T["bf", s] = k

        def norms(h):
            b = h % 2
            raw = ring[:, 4 + 2 * b:6 + 2 * b, :].rearrange("p a c -> p (a c)")
            k = dma(raw, w13[:, h, :], [T.get(("sq", h - 2))], f"d_w{b}")
            sq = hT[:, b, :, :].rearrange("p a c -> p (a c)").bitcast(BF16)
            T["sq", h] = k = act(sq, raw, ACT.Square, [k, T.get(("nm", h - 2))])
            T["nm", h] = mm([(PG[:, i * 16 + h:i * 16 + h + 1], sq[:, i * 128:(i + 1) * 128], one1[:, :], True, True)
                             for i in range(8)], [k, k_one])

        def scales():
            n2, e, s = st[:, 96:128], sti[:, 16:48], sti[:, 48:80]
            v = PG[:, 0:128].rearrange("p (w k h) -> p w h k", w=2, k=4)
            k = red(n2.rearrange("p (w h) -> p w h", w=2), v, ALU.add, [T["nm", NH - 1]])
            T["PGfree"] = k
            k = ts(n2, n2, 1e-30, 1e30, ALU.max, ALU.min, [k])
            k = ts(e, n2.bitcast(I32), 23, None, ALU.logical_shift_right, None, [k])
            k = ts(e, e, 1.0, None, ALU.add, None, [k])
            ke = ts(e, e, 1, None, ALU.logical_shift_right, None, [k])

            def power(dst, src, mul, add, waits):
                k = ts(s[:, 0:src.shape[1]], src, mul, add, ALU.mult, ALU.add, waits)
                return ts(dst.bitcast(I32), s[:, 0:src.shape[1]], 23, None, ALU.logical_shift_left, None, [k])
            s1 = st[:, 128:160]
            k = power(s1, e, -1.0, 204.0, [ke])
            kb = P.put("vector", lambda e_: e_.tensor_copy(sbf[:, :], s1), [k], "dve")
            k = power(afs[:, 0:16], e[:, 0:16], 1.0, 40.0, [kb])
            k = power(afs[:, 16:32], e[:, 0:16], -1.0, 172.0, [k])
            k = tt(e[:, 0:16], e[:, 0:16], e[:, 16:32], ALU.add, [k])
            k = power(afs[:, 32:48], e[:, 0:16], 1.0, -5.0, [k])
            T["sc"] = ts(afs[:, 32:48], afs[:, 32:48], float(np.float32(1.0 / np.sqrt(2048))), None, ALU.mult, None, [k])
            for w in range(2):
                for j in range(4):
                    k = mm([(PD[:, j, i * 128:(i + 1) * 128], sbf[:, w * 16 + j * 4 + i:w * 16 + j * 4 + i + 1].broadcast_to([128, 128]),
                             idbf[:, :], True, True) for i in range(4)], [kb, T.get("srow"), k_ibf])
                k = act(srow[:, w, :], PD[:, :, :].rearrange("p a b -> p (a b)"), ACT.Copy, [k])
                T["srow"] = k

        def fwht(j):
            b = (PG, PU)[j % 2]
            k = mm([(b[:, :], had, F0[:, j * 512:(j + 1) * 512], True, True)], [T["bf", 3], T.get(("fe", j - 2)), T["PGfree"]])
            T["fm", j] = k
            T["fe", j] = k = act(F1[:, j * 512:(j + 1) * 512], b[:, :], ACT.Copy, [k, T["sc"]], scale=afs[:, 32 + j:33 + j])
            T["mx", j] = red(afs[:, 48 + j:49 + j], F1[:, j * 512:(j + 1) * 512], ALU.max, [k], apply_absolute_value=True)

        def scale2():
            g, gi = st[:, 4:5], sti[:, 12:13]
            k = red(g, afs[:, 48:64], ALU.max, [T["mx", NH - 1]])
            k = P.put("gpsimd", lambda e: e.partition_all_reduce(st[:, 5:6], g, 128, bass.bass_isa.ReduceOp.max), [k], "pool")
            k = ts(st[:, 5:6], st[:, 5:6], 1e-30, None, ALU.max, None, [k])
            k = ts(gi, st[:, 5:6].bitcast(I32), 23, None, ALU.logical_shift_right, None, [k])
            k = ts(sti[:, 13:14], gi, -1.0, 268.0, ALU.mult, ALU.add, [k])
            k = ts(afs[:, 64:65].bitcast(I32), sti[:, 13:14], 23, None, ALU.logical_shift_left, None, [k])
            k = ts(sti[:, 14:15], gi, 1.0, -14.0, ALU.mult, ALU.add, [k])
            T["s2"] = ts(afs[:, 65:66].bitcast(I32), sti[:, 14:15], 23, None, ALU.logical_shift_left, None, [k])

        def split2(j):
            f = F1[:, j * 512:(j + 1) * 512]
            k = act(W2[:, j, 0, :], f, ACT.Copy, [T["s2"]], scale=afs[:, 64:65])
            T["W2", j] = stt(W2[:, j, 1, :], f, afs[:, 64:65], W2[:, j, 0, :], ALU.mult, ALU.subtract, [k])

        def wprep(h):
            b = h % 2
            raw = ring[:, 4 + 2 * b:6 + 2 * b, :].rearrange("p a c -> p (a c)")
            free = T["fm", NH - 1] if h < 8 else T["W2", NH - 1]
            k = dma(raw, w13[:, h, :], [T["wp", h - 2] if h >= 2 else T["sq", NH - 1]], f"d_w{b}")
            for w in range(2):
                rv = raw[:, w * 512:(w + 1) * 512].rearrange("p (k c) -> p k c", k=4)
                sv = srow[:, w, h * 128:(h + 1) * 128].unsqueeze(1).broadcast_to([128, 4, 128])
                k1 = tt(rv, rv, sv, ALU.mult, [k, T["srow"]])
                d = WA[:, h * 2048 + w * 1024:h * 2048 + (w + 1) * 1024]
                k2 = act(d[:, 0:512], raw[:, w * 512:(w + 1) * 512], ACT.Copy, [k1, free])
                T["wp", h] = tt(d[:, 512:1024], raw[:, w * 512:(w + 1) * 512], d[:, 0:512], ALU.subtract, [k2, free])

        def product(bank, n, h, w, waits, sem):
            base = h * 2048 + w * 1024
            parts = []
            for k in range(4):
                wh = WA[:, base + k * 128:base + (k + 1) * 128]
                wl = WA[:, base + 512 + k * 128:base + 512 + (k + 1) * 128]
                xa, xb_ = xnT[n % 2][:, 0, k, :], xnT[n % 2][:, 1, k, :]
                parts += [(bank[:, :], wh, xa, k == 0, False), (bank[:, :], wh, xb_, False, False),
                          (bank[:, :], wl, xa, False, k == 3)]
            return mm(parts, waits, sem)

        def gate(n, h):
            w = [T["xn", n, t] for t in range(4)] + ([T["wp", h]] if n == 0 else [])
            T["G"] = product(PG, n, h, 0, w + [T.get("silu"), T["fe", NH - 2]], "g")
            T["silu"] = act(sil[:, :], PG[:, :], ACT.Silu, [T["G"], T.get("hd")], "silu", scale=afs[:, h:h + 1])

        def up(n, h):
            b = h % 2
            T["U"] = product(PU, n, h, 1, [T.get("hd"), T["fe", NH - 1]], "u")
            if h == NH - 1:
                T["Uend", n] = T["U"]
            T["hd"] = stt(hd[:, :], PU[:, :], afs[:, 16 + h:17 + h], sil[:, :], ALU.mult, ALU.mult,
                          [T["U"], T["silu"], T.get("hi"), T.get(("lo", 1 - b))], "hd")
            T["hi"] = act(hT[:, b, 0, :], hd[:, :], ACT.Copy, [T["hd"], T.get(("D", b))], "hi")
            T["lo", b] = tt(hT[:, b, 1, :], hd[:, :], hT[:, b, 0, :], ALU.subtract, [T["hi"], T.get(("D", b))], "lo")

        def down(n, h):
            b = h % 2
            parts = []
            for t in range(4):
                a, z = hT[:, b, 0, t * 128:(t + 1) * 128], hT[:, b, 1, t * 128:(t + 1) * 128]
                parts += [(PD[:, t, :], a, W2[:, h, 0, :], h == 0, False), (PD[:, t, :], a, W2[:, h, 1, :], False, False),
                          (PD[:, t, :], z, W2[:, h, 0, :], False, h == NH - 1)]
            w = [T["lo", b], T["srow"]] + ([T["W2", h]] if n == 0 else []) + ([T["ev", n - 1]] if n and h == 0 else [])
            T["D", b] = mm(parts, w, "d")

        def finish(n):
            for t in range(4):
                r = (n % 2) * 4 + t
                T["ev", n] = stt(ring[:, r, :], PD[:, t, :], afs[:, 65:66], ring[:, r, :], ALU.mult, ALU.add,
                                 [T["D", (NH - 1) % 2]], "ev")
                T["store", n, t] = dma(out[(n * 4 + t) * 128:(n * 4 + t + 1) * 128, :], ring[:, r, :], [T["ev", n]], f"d_o{r}")

        small_weights()
        prep = [lambda s=s, q=q: butterfly(s, q) for s in range(4) for q in range(4)]
        prep += []
        side = [lambda h=h: norms(h) for h in range(NH)] + [scales]
        a0 = attention(0)
        main = list(a0)
        lead = []
        for i in range(max(len(prep), len(side))):
            if i < len(side):
                lead.append(side[i])
            if i < len(prep):
                lead.append(prep[i])
        lead += [lambda j=j: fwht(j) for j in range(NH)] + [scale2]
        lead += [lambda j=j: split2(j) for j in range(4)] + [lambda h=h: wprep(h) for h in range(2)]
        done = 0
        for i, f in enumerate(main):
            f()
            upto = (i + 1) * len(lead) // len(main)
            while done < upto:
                lead[done]()
                done += 1

        for n in range(NC):
            todo = []
            if n == 0:
                late = [lambda j=j: split2(j) for j in range(4, NH)]
                for h in range(2, NH):
                    todo.append(lambda h=h: [g() for g in (late[2 * (h - 2):2 * (h - 1)] + [lambda: wprep(h)])])
            if n + 1 < NC:
                todo += attention(n + 1)
            slot, used = 0, 0

            def fill():
                nonlocal slot, used
                slot += 1
                skip = 2 if n else 0
                upto = -(-(slot - skip) * len(todo) // (3 * NH - 1 - skip))
                while used < min(upto, len(todo)):
                    todo[used]()
                    used += 1
            for h in range(NH):
                gate(n, h)
                fill()
                up(n, h)
                fill()
                if h:
                    down(n, h - 1)
                elif n:
                    down(n - 1, NH - 1)
                    finish(n - 1)
                if h < NH - 1:
                    fill()
            while used < len(todo):
                todo[used]()
                used += 1
        down(NC - 1, NH - 1)
        finish(NC - 1)

        ends = [T["store", n, t] for n in (NC - 2, NC - 1) for t in range(4)]
        block = ctx.enter_context(nc.Block())

        @block.sync
        def _(eng):
            P.play("sync", eng)
            for s, v in ends:
                eng.wait_ge(P.sems[s], v)

        @block.tensor
        def _(eng):
            P.play("tensor", eng)

        @block.vector
        def _(eng):
            P.play("vector", eng)

        @block.scalar
        def _(eng):
            P.play("scalar", eng)

        @block.gpsimd
        def _(eng):
            P.play("gpsimd", eng)


def constants():
    i = np.arange(128)
    bits = np.array([bin(v).count("1") for v in range(128)])
    had = np.where(bits[i[:, None] & i[None, :]] % 2, -1.0, 1.0)
    two = np.concatenate([np.eye(64), np.eye(64)], 0)
    mask = np.where(np.arange(256)[None, :] <= i[:, None], 0.0, -1e30)
    cst = np.concatenate([had, np.eye(128), two, mask], 1).astype(np.float32)
    inv = np.float32(1) / (10000.0 ** (np.arange(0, 64, 2) / 64)).astype(np.float32)
    ang = (np.arange(1024, dtype=np.float32)[:, None] * inv[None, :]).T.astype(np.float64)
    ang = np.concatenate([ang] * 4, 0)
    return cst, np.stack([np.cos(ang), np.sin(ang)]).astype(np.float32)


def kernel(L0_attn_x, L0_attn_W_to_kv, L0_attn_W_compress, L0_attn_ln_gamma, L0_attn_ln_beta, L0_attn_W_q_comp,
           L0_attn_W_kv_comp, L0_attn_W_comp2lat, L0_attn_W_out_res, L0_attn_b_out_res, L0_ffn_W1, L0_ffn_W2, L0_ffn_W3):
    import concourse.bacc as bacc
    from concourse.bass_utils import run_bass_kernel_spmd

    a = np.asarray
    x = a(L0_attn_x).reshape(NC * 512, 512)
    xT = x.reshape(NC, 512, 4, 128).transpose(0, 3, 2, 1)
    w13 = np.stack([a(w).reshape(NH, 128, 4, 128).transpose(3, 0, 2, 1) for w in (L0_ffn_W1, L0_ffn_W3)], 2)
    w13 = w13.reshape(128, NH, 1024)
    w2 = a(L0_ffn_W2).T.reshape(NH, 128, 512).transpose(1, 0, 2).reshape(128, NH * 512)
    twice = lambda m: np.concatenate([m, m], 0)
    kv = a(L0_attn_W_kv_comp)
    wv = kv[64:128]
    col = lambda v: twice(a(v)[:, None])
    small = np.concatenate([
        a(L0_attn_W_to_kv), a(L0_attn_W_compress).T, twice(a(L0_attn_W_q_comp).T), twice(kv[0:64].T),
        twice(np.concatenate([wv, wv], 1)), a(L0_attn_W_comp2lat), a(L0_attn_W_out_res).T,
        col(L0_attn_ln_gamma), col(L0_attn_ln_beta), np.broadcast_to(a(L0_attn_b_out_res)[None, :], (128, 512))], 1)
    cst, tab = constants()
    arrays = {"x": x, "xT": xT, "w13": w13, "w2": w2, "small": small, "cst": cst, "tab": tab}
    arrays = {k: np.ascontiguousarray(v) for k, v in arrays.items()}
    nc = bacc.Bacc("TRN2", target_bir_lowering=False, num_devices=1)
    aps = {k: nc.dram_tensor(k, v.shape, mybir.dt.from_np(v.dtype), kind="ExternalInput").ap() for k, v in arrays.items()}
    out = nc.dram_tensor("out", (NC * 512, 512), F32, kind="ExternalOutput").ap()
    build_kernel(nc, out=out, **aps)
    r = run_bass_kernel_spmd(nc, [arrays], core_ids=[0])
    return r.results[0]["out"].reshape(8, 1024, 512)
```

```python
from contextlib import ExitStack

import numpy as np
import concourse.bass as bass
from concourse import mybir

F32 = mybir.dt.float32
F32R = mybir.dt.float32r
F16 = mybir.dt.float16
BF16 = mybir.dt.bfloat16
I32 = mybir.dt.int32
ALU = mybir.AluOpType
ACT = mybir.ActivationFunctionType
AX = mybir.AxisListType

NC = 16
NH = 16
EPS = 1e-5
WTK, WCT, WQ, WK, WV, WCL, WOR, GB, BIAS, NSM = 0, 512, 576, 640, 704, 832, 896, 1408, 1410, 1922
HAD, IDN, IDD, MSK, NCST = 0, 128, 256, 320, 576


class Program:

    ENG = ("tensor", "vector", "scalar", "gpsimd", "sync")

    def __init__(self, nc, ctx):
        self.nc, self.ctx = nc, ctx
        self.queue = {e: [] for e in self.ENG}
        self.sems, self.count = {}, {}

    def sem(self, name):
        if name not in self.sems:
            self.sems[name] = self.ctx.enter_context(self.nc.semaphore(name))
            self.count[name] = 0
        return self.sems[name]

    def put(self, eng, fn, waits, sem, by=1):
        self.sem(sem)
        self.count[sem] += by
        self.queue[eng].append((fn, [w for w in waits if w is not None], sem, by))
        return sem, self.count[sem]

    def play(self, eng_name, eng):
        seen = {}
        for fn, waits, sem, by in self.queue[eng_name]:
            for s, v in waits:
                if seen.get(s, 0) < v:
                    eng.wait_ge(self.sems[s], v)
                    seen[s] = v
            fn(eng).then_inc(self.sems[sem], by)


def build_kernel(nc, x, xT, w13, w2, small, cst, tab, out):
    with ExitStack() as ctx:
        P = Program(nc, ctx)

        def sb(name, shape, dt):
            return ctx.enter_context(nc.sbuf_tensor(name, shape, dt))

        WA = sb("WA", [128, NH * 2048], F16)
        W2 = sb("W2s", [128, NH, 2, 512], F16)
        ring = sb("ring", [128, 8, 512], F32)
        xnT = [sb(f"xnT{i}", [128, 2, 4, 512], F16) for i in range(2)]
        sil = sb("sil", [128, 512], F32)
        hd = sb("hd", [128, 512], F32)
        hT = sb("hT", [128, 2, 2, 512], F16)
        cosT = sb("cosT", [128, 1024], F32)
        sinT = sb("sinT", [128, 1024], F32)
        Q = sb("Q", [128, 512], F32R)
        Kh = sb("Kh", [128, 1024], F32R)
        Kl = sb("Kl", [128, 1024], F32R)
        V = sb("V", [128, 8, 128], F16)
        xraw = sb("xraw", [128, 2, 512], F32)
        xh = sb("xh", [128, 512], F32R)
        xl = sb("xl", [128, 512], F32R)
        VT = sb("VT", [128, 512], F32R)
        xs = sb("xs", [128, 512], F32)
        xnp = sb("xnp", [128, 2, 512], F16)
        PB = sb("PB", [128, 1024], F32)
        Ph = sb("Ph", [128, 1024], F16)
        Pl = sb("Pl", [128, 1024], F16)
        PT = sb("PT", [128, 2, 1024], F16)
        oh = sb("oh", [128, 128], F32R)
        ol = sb("ol", [128, 128], F32R)
        Mh = sb("Mh", [128, 512], F32R)
        Ml = sb("Ml", [128, 512], F32R)
        bb = sb("bb", [128, 512], F32)
        Wc = sb("Wc", [128, 4, 128], F32R)
        Wph = sb("Wph", [128, 4, 128], F32R)
        Wpl = sb("Wpl", [128, 4, 128], F32R)
        cs = sb("cst_s", [128, NCST], F32)
        id16 = sb("id16", [128, 128], F16)
        raw = sb("raw", [128, 2, 1024], F32)
        nhad = sb("nhad", [128, 128], F32)
        st = sb("st", [128, 160], F32)
        sti = sb("sti", [128, 160], I32)
        afs = sb("afs", [128, 80], F32)
        pbias = sb("pbias", [128, 4], F32)

        xTc = xs
        wsm = xnT[1][:, :, :, :].rearrange("p a b c -> p (a b c)").bitcast(F32)
        wn = xnT[1][:, :, :, :].rearrange("p a b c -> p (a b c)")
        Fw = WA[:, :].bitcast(F32)
        F0, F1 = Fw[:, 0:8192], Fw[:, 8192:16384]

        XY = ctx.enter_context(nc.psum_tensor("XY", [128, 1024], F32))
        PG = ctx.enter_context(nc.psum_tensor("PG", [128, 512], F32))
        PU = ctx.enter_context(nc.psum_tensor("PU", [128, 512], F32))
        PD = ctx.enter_context(nc.psum_tensor("PD", [128, 4, 512], F32))
        X, Y = XY[:, 0:512], XY[:, 512:1024]
        X16, Y16 = X.bitcast(F16), Y.bitcast(F16)

        had, idn = cs[:, HAD:HAD + 128], cs[:, IDN:IDN + 128]
        idd, msk = cs[:, IDD:IDD + 64], cs[:, MSK:MSK + 256]
        gam, bet = wsm[:, GB:GB + 1], wsm[:, GB + 1:GB + 2]

        def mm(parts, waits, sem="pe"):
            def go(e):
                for o, l, r, a, z in parts:
                    last = e.matmul(o, l, r, start=a, stop=z)
                return last
            return P.put("tensor", go, waits, sem)

        def tr(parts, ident, waits, sem="pe"):
            def go(e):
                for o, i in parts:
                    last = e.transpose(o, i, ident)
                return last
            return P.put("tensor", go, waits, sem)

        def act(o, i, func, waits, sem="act", **kw):
            return P.put("scalar", lambda e: e.activation(o, i, func, **kw), waits, sem)

        def tt(o, a, b, op, waits, sem="dve", eng="vector"):
            return P.put(eng, lambda e: e.tensor_tensor(o, a, b, op), waits, sem)

        def ts(o, a, s1, s2, op0, op1, waits, sem="dve"):
            if op1 is None:
                return P.put("vector", lambda e: e.tensor_scalar(o, a, s1, None, op0), waits, sem)
            return P.put("vector", lambda e: e.tensor_scalar(o, a, s1, s2, op0, op1), waits, sem)

        def stt(o, a, s, b, op0, op1, waits, sem="dve"):
            return P.put("vector", lambda e: e.scalar_tensor_tensor(o, a, s, b, op0, op1), waits, sem)

        def red(o, i, op, waits, sem="dve", **kw):
            return P.put("vector", lambda e: e.tensor_reduce(o, i, AX.X, op, **kw), waits, sem)

        def dma(o, i, waits, sem):
            return P.put("sync", lambda e: e.dma_start(o, i), waits, sem, 16)

        def rsqrt(v, y, t, ti, waits):
            k = ts(ti, v.bitcast(I32), 1, None, ALU.logical_shift_right, None, waits)
            kv = ts(v, v, -0.5, None, ALU.mult, None, [k])
            k = ts(y.bitcast(I32), ti, -1.0, 1597463007.0, ALU.mult, ALU.add, [k])
            one = y.shape[1] == 1
            for _ in range(3):
                if one:
                    k = ts(t, y, y, v, ALU.mult, ALU.mult, [k, kv])
                    k = ts(y, t, 1.5, y, ALU.add, ALU.mult, [k])
                else:
                    k = tt(t, y, y, ALU.mult, [k])
                    k = tt(t, t, v, ALU.mult, [k, kv])
                    k = stt(y, t, 1.5, y, ALU.add, ALU.mult, [k])
            return k

        T = {}
        T["Xfree"] = T["Yfree"] = None

        k_sm = dma(wsm[:, 0:NSM], small, [], "d_small")
        k_cst = dma(cs[:, :], cst, [], "d_cst")
        k_tab = [dma(t[:, :], tab[i], [], f"d_tab{i}") for i, t in enumerate((cosT, sinT))]

        def load_x(n):
            for t in range(4):
                r = (n % 2) * 4 + t
                w = [T["store", n - 2, t]] if n >= 2 else []
                T["x", n, t] = dma(ring[:, r, :], x[(n * 4 + t) * 128:(n * 4 + t + 1) * 128, :], w, f"d_x{r}")

        def load_xT(n, k):
            w = [T["xl", n, k - 2]] if k >= 2 else ([T["xl", n - 1, k + 2]] if n else [])
            T["xT", n, k] = dma(xraw[:, k % 2, :], xT[n, :, k, :], w, f"d_xT{k % 2}")

        load_xT(0, 0)
        load_xT(0, 1)
        load_x(0)
        for q in range(4):
            T["w2", q] = dma(F0[:, q * 2048:(q + 1) * 2048], w2[:, q * 2048:(q + 1) * 2048], [], f"d_w2{q}")

        k_i16 = act(id16[:, :], idn, ACT.Copy, [k_cst])
        k_nh = act(nhad[:, :], had, ACT.Copy, [k_cst], scale=-1.0)

        def small_weights():
            m1, m2 = st[:, 0:1], st[:, 1:2]
            k1 = red(m1, wsm[:, WTK:WTK + 512], ALU.add, [k_sm])
            k1 = ts(m1, m1, 1.0 / 512, None, ALU.mult, None, [k1])
            kt = ts(PB[:, 0:512], wsm[:, WTK:WTK + 512], m1, None, ALU.subtract, None, [k1])
            k2 = red(m2, wsm[:, WCT:WCT + 64], ALU.add, [k_sm])
            k2 = ts(m2, m2, 1.0 / 64, None, ALU.mult, None, [k2])
            kc = ts(PB[:, 512:576], wsm[:, WCT:WCT + 64], m2, None, ALU.subtract, None, [k2])
            km = mm([(X[:, k * 64:(k + 1) * 64], PB[:, k * 128:(k + 1) * 128], PB[:, 512:576], True, True)
                     for k in range(4)], [kt, kc])
            assert T.pop("Xfree") is None and T.pop("Yfree") is None
            xv = X[:, 0:256].rearrange("p (k c) -> p k c", k=4)
            kh = act(Wc[:, :, 0:64], xv, ACT.Copy, [km])
            T["Wc"] = tt(Wc[:, :, 64:128], xv, Wc[:, :, 0:64].bitcast(F32), ALU.subtract, [kh])
            wf = PB[:, 0:512].rearrange("p (i c) -> p i c", i=4)
            ks = [km]
            for i, base in ((0, WQ), (2, WK)):
                for h in range(2):
                    src = wsm[:, base:base + 64]
                    ks.append(ts(wf[:, i, h * 64:h * 64 + 64], src, 1.0, None, ALU.mult, None, [k_sm, km]))
                    ks.append(ts(wf[:, i + 1, h * 64:h * 64 + 32], src[:, 32:64], -1.0, None, ALU.mult, None, [km]))
                    ks.append(ts(wf[:, i + 1, h * 64 + 32:h * 64 + 64], src[:, 0:32], 1.0, None, ALU.mult, None, [km]))
            kb = mm([(Y[:, i:i + 1], wf[0:64, i, :], bet[0:64, :], True, True) for i in range(4)], [ks[-1]])
            T["pbias"] = P.put("vector", lambda e: e.tensor_copy(pbias[:, :], Y[:, 0:4]), [kb], "dve")
            wg = xs[:, :].rearrange("p (i c) -> p i c", i=4)
            kg = ts(wg, wf, gam, None, ALU.mult, None, [ks[-1]])
            kh = act(Wph[:, :, :], wg, ACT.Copy, [kg])
            T["Wp"] = tt(Wpl[:, :, :], wg, Wph[:, :, :].bitcast(F32), ALU.subtract, [kh])
            ka = tt(PB[:, 512:1024], wsm[:, WTK:WTK + 512], wsm[:, WOR:WOR + 512], ALU.add, [k_sm, km])
            k1 = mm([(Y[0:64, :], wsm[:, WCL:WCL + 64], PB[:, 512:1024], True, True)], [ka, T["pbias"]])
            k1 = act(PB[0:64, 0:512], Y[0:64, :], ACT.Copy, [k1, T["Wp"], kb])
            k1 = mm([(X, wsm[0:64, WV:WV + 128], PB[0:64, 0:512], True, True)], [k1, T["Wc"]])
            kM = act(PB[:, 512:1024], X, ACT.Copy, [k1])
            kb = mm([(Y, bet[0:64, :].broadcast_to([64, 128]), PB[0:64, 512:1024], True, True)], [kM, k1])
            T["bb"] = tt(bb[:, :], Y, wsm[:, BIAS:BIAS + 512], ALU.add, [kb])
            kg = ts(PB[:, 0:512], PB[:, 512:1024], gam, None, ALU.mult, None, [kM])
            kh = act(Mh[:, :], PB[:, 0:512], ACT.Copy, [kg])
            T["Xfree"], T["Yfree"] = kM, T["bb"]
            T["M"] = tt(Ml[:, :], PB[:, 0:512], Mh[:, :].bitcast(F32), ALU.subtract, [kh])

        def attention(n):
            c, first = n % 2, n == 0
            pos = c * 512

            def stats():
                if n:
                    load_x(n)

            def xstats():
                for t in range(4):
                    r = (n % 2) * 4 + t
                    k = P.put("vector", lambda e, t=t, r=r: e.bn_stats(st[:, 8 + 6 * t:14 + 6 * t], ring[:, r, :]),
                              [T["x", n, t]], "dve")
                    T["xs1", n, t] = k
                for t in range(4):
                    r = (n % 2) * 4 + t
                    k = P.put("vector", lambda e, t=t: e.bn_aggr(st[:, 32 + 2 * t:34 + 2 * t], st[:, 8 + 6 * t:14 + 6 * t]),
                              [T["xs1", n, t]], "dve")
                    T["xb", n, t] = tt(ring[:, r, :], ring[:, r, :], bb[:, :], ALU.add,
                                       [T["xs1", n, t], T["bb"]], "pool", "gpsimd")
                T["xst", n] = k

            def conv(k):
                def go():
                    w = [T["xT", n, k], T["cp", n, k - 1] if k else T.get(("cp", n - 1, 3))]
                    T["xh", n, k] = act(xh[:, :], xraw[:, k % 2, :], ACT.Copy, w)
                    T["xl", n, k] = tt(xl[:, :], xraw[:, k % 2, :], xh[:, :].bitcast(F32), ALU.subtract,
                                       [T["xh", n, k], w[1]])
                    if k < 2:
                        load_xT(n, k + 2)
                return go

            def cproj(k):
                def go():
                    T["cp", n, k] = mm([(X, Wc[:, k, :], xh[:, :], k == 0, False),
                                        (X, Wc[:, k, :], xl[:, :], False, k == 3)],
                                       [T["xl", n, k], T["Wc"]] + ([T.pop("Xfree")] if k == 0 else []))
                return go

            def latent():
                T["cT"] = act(xTc[:, :], X, ACT.Copy, [T["cp", n, 3], T.get("xsfree"), T.get("Wp")])
                T["Xfree"] = T["cT"]

            def latent2():
                T["ct"] = mm([(Y[:, t * 64:t * 64 + 64], xTc[:, t * 128:(t + 1) * 128], idd, True, True)
                              for t in range(4)], [T["cT"], T.pop("Yfree"), k_cst])
                c0 = PB[:, 0:256]
                T["c0"] = T["Yfree"] = act(c0, Y[:, 0:256], ACT.Copy, [T["ct"], T.get("PBfree"), T.get("M"), T.get("Ph")])

            def norm1():
                c0, c1 = PB[:, 0:256], PB[:, 256:512]
                c3 = c0.rearrange("p (t c) -> p t c", t=4)
                k = tt(c1, c0, c0, ALU.mult, [T["c0"], T.get("PBfree"), T.get("M")])
                k = red(st[:, 40:44], c1.rearrange("p (t c) -> p t c", t=4), ALU.add, [k])
                var = st[:, 32:40].rearrange("p (t c) -> p t c", t=4)[:, :, 1]
                k2 = ts(st[:, 44:48], var, EPS, EPS * EPS, ALU.mult, ALU.add, [T["xst", n]])
                k = stt(st[:, 48:52], st[:, 40:44], 1.0 / 64, st[:, 44:48], ALU.mult, ALU.add, [k, k2])
                k = rsqrt(st[:, 48:52], st[:, 52:56], st[:, 56:60], sti[:, 0:4], [k])
                k = ts(st[:, 52:56], st[:, 52:56], 256.0, None, ALU.mult, None, [k])
                cn = c1.rearrange("p (t c) -> p t c", t=4)
                k = tt(cn, c3, st[:, 52:56].unsqueeze(2).broadcast_to([128, 4, 64]), ALU.mult, [k])
                vh, vl = V[:, 4 * c:4 * c + 4, 0:64], V[:, 4 * c:4 * c + 4, 64:128]
                k = P.put("vector", lambda e: e.tensor_copy(vh, cn), [k, T.get("PVlast")], "dve")
                T["V", n] = tt(vl, cn, vh, ALU.subtract, [k])

            def vT():
                k = tr([(X16[:, t * 128:(t + 1) * 128], V[:, 4 * c + t, :]) for t in range(4)], id16[:, :],
                       [T["V", n], T.pop("Xfree"), k_i16])
                T["VT"] = act(VT[:, :], X16[:, 0:512], ACT.Copy, [k, T.get("VTfree")], scale=1.0 / 256)
                T["Xfree"] = T["VT"]

            def proj(i):
                def go():
                    T["pj", i] = mm([(X, Wph[:, i, :], VT[:, :], True, False), (X, Wpl[:, i, :], VT[:, :], False, True),
                                     (Y, Wph[:, i + 1, :], VT[:, :], True, False), (Y, Wpl[:, i + 1, :], VT[:, :], False, True)],
                                    [T["VT"], T.pop("Xfree"), T.pop("Yfree"), T["Wp"]])
                    T["VTfree"] = T["pj", i]
                    a, b = PB[:, 0:512], PB[:, 512:1024]
                    ka = stt(a, X, pbias[:, i:i + 1], cosT[:, pos:pos + 512], ALU.add, ALU.mult,
                             [T["pj", i], T["V", n], T.get("rope"), T["pbias"], k_tab[0]])
                    T["Xfree"] = ka
                    kb = stt(b, Y, pbias[:, i + 1:i + 2], sinT[:, pos:pos + 512], ALU.add, ALU.mult,
                             [T["pj", i], T.get("rope"), T.get("PBfree"), k_tab[1]])
                    T["Yfree"] = kb
                    k = tt(a, a, b, ALU.add, [ka, kb])
                    if i == 0:
                        kq = act(Q[:, :], a, ACT.Copy, [k, T.get("Qfree")])
                        T["Q"] = tt(Q[64:128, :], a[64:128, :], Q[64:128, :].bitcast(F32), ALU.subtract, [kq])
                    else:
                        kk = act(Kh[:, pos:pos + 512], a, ACT.Copy, [k, T.get("Qfree")])
                        T["K"] = tt(Kl[:, pos:pos + 512], a, Kh[:, pos:pos + 512].bitcast(F32), ALU.subtract, [kk])
                    T["rope"] = T["Q"] if i == 0 else T["K"]
                return go

            def tile(ti):
                t, ns = ti % 4, ti + 1
                W = max(256, ns * 128)
                r = (n % 2) * 4 + t
                q = Q[:, t * 128:(t + 1) * 128]
                c_ = 64 + 8 * (ti % 2)
                nmax, rsum, rinv = st[:, c_:c_ + 1], st[:, c_ + 1:c_ + 2], st[:, c_ + 2:c_ + 3]

                def scores():
                    parts = []
                    for a in range(0, W, 512):
                        z = min(W, a + 512)
                        if z - a < 256:
                            z = a + 256
                        parts += [(XY[:, a:z], q, Kh[:, a:z], True, False), (XY[:, a:z], q, Kl[:, a:z], False, True)]
                    w = [T["Q"], T["K"], T.pop("Xfree")] + ([T.pop("Yfree")] if W > 512 else [])
                    k = mm(parts, w)
                    T["Qfree"] = k
                    d = (ns - 1) * 128
                    k = tt(XY[:, d:d + 128], XY[:, d:d + 128], msk[:, 0:128], ALU.add, [k])
                    k = red(rsum, XY[:, 0:ns * 128], ALU.max, [k, T.get(("rinv", ti % 2))])
                    T["nmax"] = ts(nmax, rsum, -0.125, None, ALU.mult, None, [k, T.get(("exp", ti % 2))])

                def exps():
                    w = ns * 128
                    k = P.put("scalar", lambda e: e.activation(PB[:, 0:w], XY[:, 0:w], ACT.Exp, bias=nmax, scale=0.125,
                                                               accum_out=rsum), [T["nmax"], T.get("Pl"), T["rope"]], "act")
                    T["exp", ti % 2] = k
                    T["Xfree"] = k
                    if w > 512:
                        T["Yfree"] = k
                    T["Ph"] = act(Ph[:, 0:w], PB[:, 0:w], ACT.Copy, [k, T.get("Tlast")], scale=4096.0)

                def low():
                    w = ns * 128
                    T["Pl"] = stt(Pl[:, 0:w], PB[:, 0:w], 4096.0, Ph[:, 0:w], ALU.mult, ALU.subtract, [T["Ph"], T.get("Tlast")])
                    T["PBfree"] = T["Pl"]
                    k = ts(rinv, rsum, float(2 ** 20), None, ALU.mult, None, [T["exp", ti % 2], T.get(("x2", ti % 2))])
                    T["rinv", ti % 2] = P.put("vector", lambda e: e.reciprocal(rinv, rinv), [k], "dve")

                def trans(g):
                    s0, s1 = 4 * g, min(ns, 4 * g + 4)
                    m = s1 - s0
                    k = tr([(Y16[:, (h * m + s) * 128:(h * m + s + 1) * 128], (Ph, Pl)[h][:, (s0 + s) * 128:(s0 + s + 1) * 128])
                            for h in range(2) for s in range(m)], id16[:, :], [T["Pl"], T.pop("Yfree")])
                    T["Tlast"] = k
                    k = act(PT[:, g, 0:2 * m * 128], Y16[:, 0:2 * m * 128], ACT.Copy, [k, T.get(("PVg", g))])
                    T["Yfree"] = T["PT", g] = k

                def pv(g):
                    s0, s1 = 4 * g, min(ns, 4 * g + 4)
                    m = s1 - s0
                    parts = [(X[:, 0:128], V[:, s0 + s, :], PT[:, g, (h * m + s) * 128:(h * m + s + 1) * 128],
                              s0 + s == 0 and h == 0, s0 + s == ns - 1 and h == 1)
                             for s in range(m) for h in range(2)]
                    k = mm(parts, [T["PT", g]] + ([T.pop("Xfree")] if g == 0 else []))
                    T["PVg", g] = T["PVlast"] = k
                    if s1 == ns:
                        k = P.put("vector", lambda e: e.tensor_copy(oh[:, :], X[:, 0:128]), [k, T.get("opm")], "dve")
                        T["o"] = T["Xfree"] = tt(ol[:, :], X[:, 0:128], oh[:, :].bitcast(F32), ALU.subtract, [k])

                def outp():
                    T["opm"] = k = mm([(Y, oh[:, :], Mh[:, :], True, False), (Y, oh[:, :], Ml[:, :], False, False),
                                       (Y, ol[:, :], Mh[:, :], False, True)], [T["o"], T.pop("Yfree"), T["M"]])
                    xt = ring[:, r, :]
                    k = stt(xt, Y, rinv, xt, ALU.mult, ALU.add, [k, T["rinv", ti % 2], T["xb", n, t]])
                    T["x2", ti % 2] = T["Yfree"] = k
                    k = P.put("vector", lambda e: e.bn_stats(st[:, 80:86], xt), [k], "dve")
                    k = P.put("vector", lambda e: e.bn_aggr(st[:, 86:88], st[:, 80:86]), [k], "dve")
                    k = ts(st[:, 88:89], st[:, 87:88], EPS, None, ALU.add, None, [k])
                    k = rsqrt(st[:, 88:89], st[:, 89:90], st[:, 90:91], sti[:, 8:9], [k])
                    k = ts(st[:, 89:90], st[:, 89:90], 1024.0, None, ALU.mult, None, [k])
                    k = ts(xs[:, :], xt, st[:, 86:87], st[:, 89:90], ALU.subtract, ALU.mult, [k, T.get("xh16"), T["ct"]])
                    T["xh16"] = act(xnp[:, 0, :], xs[:, :], ACT.Copy, [k, T.get("XT")])
                    T["xn16"] = tt(xnp[:, 1, :], xs[:, :], xnp[:, 0, :], ALU.subtract, [T["xh16"], T.get("XT")])
                    T["xsfree"] = T["xn16"]

                def xtr():
                    T["XT"] = k = tr([(X16[:, (h * 4 + j) * 128:(h * 4 + j + 1) * 128], xnp[:, h, j * 128:(j + 1) * 128])
                                      for h in range(2) for j in range(4)], id16[:, :], [T["xn16"], T.pop("Xfree")])
                    k = act(xnT[n % 2][:, :, :, t * 128:(t + 1) * 128], X16.rearrange("p (h j c) -> p h j c", h=2, j=4),
                            ACT.Copy, [k, T.get(("Uend", n - 2))] + ([T["wt", NH - 1]] if n == 1 else []))
                    T["Xfree"] = T["xn", n, t] = k

                b = 14 + 7 * t
                plan = [(b, scores), (b + 1, exps), (b + 2, low), (b + 3, lambda: trans(0)), (b + 4, lambda: pv(0)),
                        (b + 6, outp), (b + 10, xtr)]
                if ns > 4:
                    plan += [(b + 4, lambda: trans(1)), (b + 5, lambda: pv(1))]
                return plan

            plan = [(0, conv(0)), (3, stats), (5, latent), (5, latent2), (7, xstats), (7, norm1), (10, vT), (11, proj(2)), (12, proj(0))]
            for k in range(4):
                plan.append((k + 1, cproj(k)))
                if k < 3:
                    plan.append((k + 1, conv(k + 1)))
            for ti in range(4 * c, 4 * c + 4):
                plan += tile(ti)
            return sorted(plan, key=lambda s: s[0])

        def butterfly(q):
            a, b = F0[:, q * 2048:(q + 1) * 2048], F1[:, q * 2048:(q + 1) * 2048]
            for s, (src, dst) in enumerate(((a, b), (b, a))):
                pat = "p (g two n) -> p two g n" if s == 0 else "p (two g n) -> p two g n"
                u, v = src.rearrange(pat, two=2, n=512), dst.rearrange(pat, two=2, n=512)
                w = [T["w2", q]] if s == 0 else [k0, k]
                k0 = tt(v[:, 0], u[:, 0], u[:, 1], ALU.add, w)
                k = tt(v[:, 1], u[:, 0], u[:, 1], ALU.subtract, w)
            T["bf", q] = k

        def norms(h):
            b = h % 2
            k = dma(raw[:, b, :], w13[:, h, :], [T.get(("nm", h - 2))], f"d_w{b}")
            for w in range(2):
                junk = hT[:, b, w, :].bitcast(BF16)
                c = 96 + w * 16 + h
                T["nm", h] = P.put("scalar", lambda e, w=w, junk=junk, c=c: e.activation(
                    junk, raw[:, b, w * 512:(w + 1) * 512], ACT.Square, accum_out=st[:, c:c + 1]), [k, T.get(("nm", h - 2))], "act")

        def scales():
            n2, e, s = st[:, 96:128], sti[:, 16:48], sti[:, 48:80]
            k = ts(n2, n2, 1e-30, 1e30, ALU.max, ALU.min, [T["nm", NH - 1]])
            k = ts(e, n2.bitcast(I32), 23, None, ALU.logical_shift_right, None, [k])
            k = ts(e, e, 1.0, None, ALU.add, None, [k])
            ke = ts(e, e, 1, None, ALU.logical_shift_right, None, [k])

            def power(dst, src, mul, add, waits):
                k = ts(s[:, 0:src.shape[1]], src, mul, add, ALU.mult, ALU.add, waits)
                return ts(dst.bitcast(I32), s[:, 0:src.shape[1]], 23, None, ALU.logical_shift_left, None, [k])
            k = power(st[:, 128:160], e, -1.0, 204.0, [ke])
            k = power(afs[:, 0:16], e[:, 0:16], 1.0, 40.0, [k])
            k = power(afs[:, 16:32], e[:, 0:16], -1.0, 172.0, [k])
            k = tt(e[:, 0:16], e[:, 0:16], e[:, 16:32], ALU.add, [k])
            k = power(afs[:, 32:48], e[:, 0:16], 1.0, -5.0, [k])
            T["sc"] = ts(afs[:, 32:48], afs[:, 32:48], float(np.float32(1.0 / np.sqrt(2048))), None, ALU.mult, None, [k])

        def fwht(j):
            b = (PG, PU)[j % 2]
            lo, hi = j % 4, j // 4
            parts = [(b[:, :], (had, nhad[:, :])[bin(hi & q).count("1") % 2], F0[:, (4 * q + lo) * 512:(4 * q + lo + 1) * 512],
                      q == 0, q == 3) for q in range(4)]
            T["fm", j] = k = mm(parts, [T["bf", q] for q in range(4)] + [T.get(("fe", j - 2)), k_nh])
            T["fe", j] = k = act(F1[:, j * 512:(j + 1) * 512], b[:, :], ACT.Copy, [k, T["sc"]], scale=afs[:, 32 + j:33 + j])
            T["mx", j] = P.put("scalar", lambda e: e.activation(hT[:, 0, 0, :].bitcast(BF16), F1[:, j * 512:(j + 1) * 512], ACT.Square,
                                                               accum_out=afs[:, 48 + j:49 + j]), [k, T.get(("mx", j - 1)), T["nm", NH - 1]], "act")

        def scale2():
            g, e_ = st[:, 4:5], sti[:, 12:13]
            k = red(g, afs[:, 48:64], ALU.max, [T["mx", NH - 1]])
            k = P.put("gpsimd", lambda e: e.partition_all_reduce(st[:, 5:6], g, 128, bass.bass_isa.ReduceOp.max), [k], "pool")
            k = ts(st[:, 5:6], st[:, 5:6], 1e-30, 1e30, ALU.max, ALU.min, [k])
            k = ts(e_, st[:, 5:6].bitcast(I32), 23, None, ALU.logical_shift_right, None, [k])
            k = ts(e_, e_, 1.0, None, ALU.add, None, [k])
            k = ts(e_, e_, 1, None, ALU.logical_shift_right, None, [k])
            k = ts(sti[:, 13:14], e_, -1.0, 205.0, ALU.mult, ALU.add, [k])
            k = ts(afs[:, 64:65].bitcast(I32), sti[:, 13:14], 23, None, ALU.logical_shift_left, None, [k])
            k = ts(sti[:, 14:15], e_, 1.0, 49.0, ALU.mult, ALU.add, [k])
            T["s2"] = ts(afs[:, 65:66].bitcast(I32), sti[:, 14:15], 23, None, ALU.logical_shift_left, None, [k])

        def split2(j):
            f = F1[:, j * 512:(j + 1) * 512]
            k = act(W2[:, j, 0, :], f, ACT.Copy, [T["s2"]], scale=afs[:, 64:65])
            T["W2", j] = stt(W2[:, j, 1, :], f, afs[:, 64:65], W2[:, j, 0, :], ALU.mult, ALU.subtract, [k])

        def wload(h):
            T["wl", h] = dma(raw[:, h % 2, :], w13[:, h, :], [T["wn", h - 2] if h >= 2 else T["nm", NH - 1]], f"d_w{h % 2}")

        def wsplit(h):
            b = h % 2
            for w in range(2):
                r = raw[:, b, w * 512:(w + 1) * 512]
                d = wn[:, b * 2048 + w * 1024:b * 2048 + (w + 1) * 1024]
                s1 = st[:, 128 + w * 16 + h:129 + w * 16 + h]
                k = act(d[:, 0:512], r, ACT.Copy, [T["wl", h], T["sc"], T["bb"], T["M"], T["Wp"], T.get(("wt", h - 2))], scale=s1)
                T["wn", h] = stt(d[:, 512:1024], r, s1, d[:, 0:512], ALU.mult, ALU.subtract, [k, T.get(("wt", h - 2))])

        def wtrans(h):
            b = h % 2
            free = T["fm", NH - 1] if h < 8 else T["W2", 2 * h - 15]
            for w in range(2):
                k = tr([(Y16[:, i * 128:(i + 1) * 128], wn[:, b * 2048 + w * 1024 + i * 128:b * 2048 + w * 1024 + (i + 1) * 128])
                        for i in range(8)], id16[:, :], [T["wn", h], T.pop("Yfree"), k_i16])
                T["wt", h] = k
                d = WA[:, h * 2048 + w * 1024:h * 2048 + (w + 1) * 1024]
                if w:
                    k = act(d, Y16, ACT.Copy, [k, free])
                else:
                    k = P.put("vector", lambda e, d=d: e.tensor_copy(d, Y16), [k, free], "dve")
                T["Yfree"] = T["wp", h, w] = k

        def product(bank, n, h, w, waits, sem):
            base = h * 2048 + w * 1024
            parts = []
            for k in range(4):
                wh = WA[:, base + k * 128:base + (k + 1) * 128]
                wl = WA[:, base + 512 + k * 128:base + 512 + (k + 1) * 128]
                xa, xb_ = xnT[n % 2][:, 0, k, :], xnT[n % 2][:, 1, k, :]
                parts += [(bank[:, :], wh, xa, k == 0, False), (bank[:, :], wh, xb_, False, False),
                          (bank[:, :], wl, xa, False, k == 3)]
            return mm(parts, waits, sem)

        def gate(n, h):
            w = [T["xn", n, t] for t in range(4)] + ([T["wp", h, 0]] if n == 0 else [])
            T["G"] = product(PG, n, h, 0, w + [T.get("silu"), T["fe", NH - 2]], "g")
            T["silu"] = act(sil[:, :], PG[:, :], ACT.Silu, [T["G"], T.get("hd")], "silu", scale=afs[:, h:h + 1])

        def up(n, h):
            b = h % 2
            T["U"] = product(PU, n, h, 1, [T.get("hd"), T["fe", NH - 1]] + ([T["wp", h, 1]] if n == 0 else []), "u")
            if h == NH - 1:
                T["Uend", n] = T["U"]
            T["hd"] = stt(hd[:, :], PU[:, :], afs[:, 16 + h:17 + h], sil[:, :], ALU.mult, ALU.mult,
                          [T["U"], T["silu"], T.get("hi"), T.get(("lo", 1 - b))], "hd")
            T["hi"] = act(hT[:, b, 0, :], hd[:, :], ACT.Copy, [T["hd"], T.get(("D", b))], "hi")
            T["lo", b] = tt(hT[:, b, 1, :], hd[:, :], hT[:, b, 0, :], ALU.subtract, [T["hi"], T.get(("D", b))], "lo")

        def down(n, h):
            b = h % 2
            parts = []
            for t in range(4):
                a, z = hT[:, b, 0, t * 128:(t + 1) * 128], hT[:, b, 1, t * 128:(t + 1) * 128]
                parts += [(PD[:, t, :], a, W2[:, h, 0, :], h == 0, False), (PD[:, t, :], a, W2[:, h, 1, :], False, False),
                          (PD[:, t, :], z, W2[:, h, 0, :], False, h == NH - 1)]
            w = [T["lo", b]] + ([T["W2", h]] if n == 0 else []) + ([T["ev", n - 1]] if n and h == 0 else [])
            T["D", b] = mm(parts, w, "d")

        def finish(n):
            for t in range(4):
                r = (n % 2) * 4 + t
                T["ev", n] = stt(ring[:, r, :], PD[:, t, :], afs[:, 65:66], ring[:, r, :], ALU.mult, ALU.add,
                                 [T["D", (NH - 1) % 2]], "ev")
                T["store", n, t] = dma(out[(n * 4 + t) * 128:(n * 4 + t + 1) * 128, :], ring[:, r, :], [T["ev", n]], f"d_o{r}")

        small_weights()
        lead = []
        for h in range(NH):
            lead.append(lambda h=h: norms(h))
            if h % 4 == 3:
                lead.append(lambda q=h // 4: butterfly(q))
        lead += [scales] + [lambda j=j: fwht(j) for j in range(NH)] + [scale2]
        lead += [lambda h=h: wload(h) for h in range(2)] + [lambda h=h: wsplit(h) for h in range(2)]
        lead += [lambda h=h: wload(h) for h in range(2, 4)] + [lambda j=j: split2(j) for j in range(2)]
        lead += [lambda h=h: wtrans(h) for h in range(2)]
        main = attention(0)
        done = 0
        for i, (_, f) in enumerate(main):
            f()
            upto = (i + 1) * len(lead) // len(main)
            while done < upto:
                lead[done]()
                done += 1
        load_xT(1, 0)
        load_xT(1, 1)

        for n in range(NC):
            plan = attention(n + 1) if n + 1 < NC else []
            if n + 2 < NC:
                plan.append((40, lambda: (load_xT(n + 2, 0), load_xT(n + 2, 1))))
            if n == 0:
                for h in range(2, NH):
                    plan.append((h - 2, lambda h=h: wsplit(h)))
                    plan.append((h - 1.5, lambda h=h: wtrans(h)))
                    if h + 2 < NH:
                        plan.append((h - 2, lambda h=h: wload(h + 2)))
                for j in range(2, NH):
                    plan.append((j - 2, lambda j=j: split2(j)))
                plan.sort(key=lambda s: s[0])
            slot = 0

            def fill():
                nonlocal slot
                while plan and plan[0][0] <= slot:
                    plan.pop(0)[1]()
                slot += 1
            for h in range(NH):
                gate(n, h)
                fill()
                up(n, h)
                fill()
                if h:
                    down(n, h - 1)
                elif n:
                    down(n - 1, NH - 1)
                    finish(n - 1)
                if h < NH - 1:
                    fill()
            assert not plan
        down(NC - 1, NH - 1)
        finish(NC - 1)

        ends = [T["store", n, t] for n in (NC - 2, NC - 1) for t in range(4)]
        block = ctx.enter_context(nc.Block())

        @block.sync
        def _(eng):
            P.play("sync", eng)
            for s, v in ends:
                eng.wait_ge(P.sems[s], v)

        @block.tensor
        def _(eng):
            P.play("tensor", eng)

        @block.vector
        def _(eng):
            P.play("vector", eng)

        @block.scalar
        def _(eng):
            P.play("scalar", eng)

        @block.gpsimd
        def _(eng):
            P.play("gpsimd", eng)


def constants():
    i = np.arange(128)
    bits = np.array([bin(v).count("1") for v in range(128)])
    had = np.where(bits[i[:, None] & i[None, :]] % 2, -1.0, 1.0)
    two = np.concatenate([np.eye(64), np.eye(64)], 0)
    mask = np.where(np.arange(256)[None, :] <= i[:, None], 0.0, -1e30)
    cst = np.concatenate([had, np.eye(128), two, mask], 1).astype(np.float32)
    inv = np.float32(1) / (10000.0 ** (np.arange(0, 64, 2) / 64)).astype(np.float32)
    ang = (np.arange(1024, dtype=np.float32)[:, None] * inv[None, :]).T.astype(np.float64)
    ang = np.concatenate([ang] * 4, 0)
    return cst, np.stack([np.cos(ang), np.sin(ang)]).astype(np.float32)


def kernel(L0_attn_x, L0_attn_W_to_kv, L0_attn_W_compress, L0_attn_ln_gamma, L0_attn_ln_beta, L0_attn_W_q_comp,
           L0_attn_W_kv_comp, L0_attn_W_comp2lat, L0_attn_W_out_res, L0_attn_b_out_res, L0_ffn_W1, L0_ffn_W2, L0_ffn_W3):
    import concourse.bacc as bacc
    from concourse.bass_utils import run_bass_kernel_spmd

    a = np.asarray
    x = a(L0_attn_x).reshape(NC * 512, 512)
    xT = x.reshape(NC, 512, 4, 128).transpose(0, 3, 2, 1)
    w13 = np.stack([a(w).reshape(NH, 128, 512).transpose(1, 0, 2) for w in (L0_ffn_W1, L0_ffn_W3)], 2)
    w13 = w13.reshape(128, NH, 1024)
    w2 = a(L0_ffn_W2).T.reshape(NH, 128, 512).transpose(1, 0, 2).reshape(128, NH * 512)
    twice = lambda m: np.concatenate([m, m], 0)
    kv = a(L0_attn_W_kv_comp)
    wv = kv[64:128]
    col = lambda v: twice(a(v)[:, None])
    small = np.concatenate([
        a(L0_attn_W_to_kv), a(L0_attn_W_compress).T, twice(a(L0_attn_W_q_comp).T), twice(kv[0:64].T),
        twice(np.concatenate([wv, wv], 1)), a(L0_attn_W_comp2lat), a(L0_attn_W_out_res).T,
        col(L0_attn_ln_gamma), col(L0_attn_ln_beta), np.broadcast_to(a(L0_attn_b_out_res)[None, :], (128, 512))], 1)
    cst, tab = constants()
    arrays = {"x": x, "xT": xT, "w13": w13, "w2": w2, "small": small, "cst": cst, "tab": tab}
    arrays = {k: np.ascontiguousarray(v) for k, v in arrays.items()}
    nc = bacc.Bacc("TRN2", target_bir_lowering=False, num_devices=1)
    aps = {k: nc.dram_tensor(k, v.shape, mybir.dt.from_np(v.dtype), kind="ExternalInput").ap() for k, v in arrays.items()}
    out = nc.dram_tensor("out", (NC * 512, 512), F32, kind="ExternalOutput").ap()
    build_kernel(nc, out=out, **aps)
    r = run_bass_kernel_spmd(nc, [arrays], core_ids=[0])
    return r.results[0]["out"].reshape(8, 1024, 512)
```

```python
from contextlib import ExitStack

import numpy as np
import concourse.bass as bass
from concourse import mybir

F32 = mybir.dt.float32
F32R = mybir.dt.float32r
F16 = mybir.dt.float16
BF16 = mybir.dt.bfloat16
I32 = mybir.dt.int32
ALU = mybir.AluOpType
ACT = mybir.ActivationFunctionType
AX = mybir.AxisListType

NC = 16
NH = 16
EPS = 1e-5
WTK, WCT, WQ, WK, WV, WCL, WOR, GB, BIAS, NSM = 0, 512, 576, 640, 704, 832, 896, 1408, 1410, 1922
HAD, IDN, IDD, MSK, NCST = 0, 128, 256, 320, 576


class Program:

    ENG = ("tensor", "vector", "scalar", "gpsimd", "sync")

    def __init__(self, nc, ctx):
        self.nc, self.ctx = nc, ctx
        self.queue = {e: [] for e in self.ENG}
        self.sems, self.count = {}, {}

    def sem(self, name):
        if name not in self.sems:
            self.sems[name] = self.ctx.enter_context(self.nc.semaphore(name))
            self.count[name] = 0
        return self.sems[name]

    def put(self, eng, fn, waits, sem, by=1):
        self.sem(sem)
        self.count[sem] += by
        self.queue[eng].append((fn, [w for w in waits if w is not None], sem, by))
        return sem, self.count[sem]

    def play(self, eng_name, eng):
        seen = {}
        for fn, waits, sem, by in self.queue[eng_name]:
            for s, v in waits:
                if seen.get(s, 0) < v:
                    eng.wait_ge(self.sems[s], v)
                    seen[s] = v
            fn(eng).then_inc(self.sems[sem], by)


def build_kernel(nc, x, xT, w13, w2, small, cst, tab, out):
    with ExitStack() as ctx:
        P = Program(nc, ctx)

        def sb(name, shape, dt):
            return ctx.enter_context(nc.sbuf_tensor(name, shape, dt))

        WA = sb("WA", [128, NH * 2048], F16)
        W2 = sb("W2s", [128, NH, 2, 512], F16)
        ring = sb("ring", [128, 8, 512], F32)
        xnT = [sb(f"xnT{i}", [128, 2, 4, 512], F16) for i in range(2)]
        sil = sb("sil", [128, 512], F32)
        hd = sb("hd", [128, 512], F32)
        hT = sb("hT", [128, 2, 2, 512], F16)
        cosT = sb("cosT", [128, 1024], F32)
        sinT = sb("sinT", [128, 1024], F32)
        Q = sb("Q", [128, 512], F32R)
        Kh = sb("Kh", [128, 1024], F32R)
        Kl = sb("Kl", [128, 1024], F32R)
        V = sb("V", [128, 8, 128], F16)
        xraw = sb("xraw", [128, 2, 512], F32)
        xh = sb("xh", [128, 512], F32R)
        xl = sb("xl", [128, 512], F32R)
        VT = sb("VT", [128, 512], F32R)
        xs = sb("xs", [128, 512], F32)
        xnp = sb("xnp", [128, 2, 512], F16)
        PB = sb("PB", [128, 1024], F32)
        Ph = sb("Ph", [128, 1024], F16)
        Pl = sb("Pl", [128, 1024], F16)
        PT = sb("PT", [128, 2, 1024], F16)
        oh = sb("oh", [128, 128], F32R)
        ol = sb("ol", [128, 128], F32R)
        Mh = sb("Mh", [128, 512], F32R)
        Ml = sb("Ml", [128, 512], F32R)
        bb = sb("bb", [128, 512], F32)
        Wc = sb("Wc", [128, 4, 128], F32R)
        Wph = sb("Wph", [128, 2, 128], F32R)
        Wpl = sb("Wpl", [128, 2, 128], F32R)
        cs = sb("cst_s", [128, NCST], F32)
        id16 = sb("id16", [128, 128], F16)
        raw = sb("raw", [128, 2, 512], F32)
        wn = sb("wn", [128, 2, 2, 512], F16)
        st = sb("st", [128, 160], F32)
        sti = sb("sti", [128, 160], I32)
        bn2 = sb("bn2", [128, NH, 6], F32)
        mv2 = sb("mv2", [128, NH, 2], F32)
        afs = sb("afs", [128, 80], F32)
        pbias = sb("pbias", [128, 2], F32)

        xTc = xs
        rows = W2[:, :, :, :].rearrange("p a b c -> p (a b c)").bitcast(F32).rearrange("p (h c) -> p h c", h=8)
        wsm = xnT[1][:, :, :, :].rearrange("p a b c -> p (a b c)").bitcast(F32)
        Fw = WA[:, :].bitcast(F32)
        F0, F1 = Fw[:, 0:8192], Fw[:, 8192:16384]

        XY = ctx.enter_context(nc.psum_tensor("XY", [128, 1024], F32))
        PG = ctx.enter_context(nc.psum_tensor("PG", [128, 512], F32))
        PU = ctx.enter_context(nc.psum_tensor("PU", [128, 512], F32))
        PD = ctx.enter_context(nc.psum_tensor("PD", [128, 4, 512], F32))
        X, Y = XY[:, 0:512], XY[:, 512:1024]
        X16, Y16 = X.bitcast(F16), Y.bitcast(F16)

        had, idn = cs[:, HAD:HAD + 128], cs[:, IDN:IDN + 128]
        idd, msk = cs[:, IDD:IDD + 64], cs[:, MSK:MSK + 256]
        gam, bet = wsm[:, GB:GB + 1], wsm[:, GB + 1:GB + 2]

        def mm(parts, waits, sem="pe"):
            def go(e):
                for o, l, r, a, z in parts:
                    last = e.matmul(o, l, r, start=a, stop=z)
                return last
            return P.put("tensor", go, waits, sem)

        def tr(parts, ident, waits, sem="pe"):
            def go(e):
                for o, i in parts:
                    last = e.transpose(o, i, ident)
                return last
            return P.put("tensor", go, waits, sem)

        def act(o, i, func, waits, sem="act", **kw):
            return P.put("scalar", lambda e: e.activation(o, i, func, **kw), waits, sem)

        def tt(o, a, b, op, waits, sem="dve", eng="vector"):
            return P.put(eng, lambda e: e.tensor_tensor(o, a, b, op), waits, sem)

        def ts(o, a, s1, s2, op0, op1, waits, sem="dve"):
            if op1 is None:
                return P.put("vector", lambda e: e.tensor_scalar(o, a, s1, None, op0), waits, sem)
            return P.put("vector", lambda e: e.tensor_scalar(o, a, s1, s2, op0, op1), waits, sem)

        def pool_ts(o, a, s1, op, waits):
            return P.put("gpsimd", lambda e: e.tensor_scalar(o, a, s1, None, op), waits, "pool")

        def stt(o, a, s, b, op0, op1, waits, sem="dve"):
            return P.put("vector", lambda e: e.scalar_tensor_tensor(o, a, s, b, op0, op1), waits, sem)

        def red(o, i, op, waits, sem="dve", **kw):
            return P.put("vector", lambda e: e.tensor_reduce(o, i, AX.X, op, **kw), waits, sem)

        def dma(o, i, waits, sem):
            return P.put("sync", lambda e: e.dma_start(o, i), waits, sem, 16)

        def rsqrt(v, y, t, ti, waits):
            k = ts(ti, v.bitcast(I32), 1, None, ALU.logical_shift_right, None, waits)
            kv = ts(v, v, -0.5, None, ALU.mult, None, [k])
            k = ts(y.bitcast(I32), ti, -1.0, 1597463007.0, ALU.mult, ALU.add, [k])
            one = y.shape[1] == 1
            for _ in range(3):
                if one:
                    k = ts(t, y, y, v, ALU.mult, ALU.mult, [k, kv])
                    k = ts(y, t, 1.5, y, ALU.add, ALU.mult, [k])
                else:
                    k = tt(t, y, y, ALU.mult, [k])
                    k = tt(t, t, v, ALU.mult, [k, kv])
                    k = stt(y, t, 1.5, y, ALU.add, ALU.mult, [k])
            return k

        T = {}
        T["Xfree"] = T["Yfree"] = None

        def load_x(n):
            for t in range(4):
                r = (n % 2) * 4 + t
                w = [T["store", n - 2, t]] if n >= 2 else ([T["bb"], T["M"]] if n else [])
                T["x", n, t] = dma(ring[:, r, :], x[(n * 4 + t) * 128:(n * 4 + t + 1) * 128, :], w, f"d_x{r}")

        def xsrc(n, k):
            return (sil, hd)[k - 2][:, :] if n == 0 and k >= 2 else xraw[:, k % 2, :]

        def load_xT(n, k):
            if n == 0:
                T["xT", n, k] = dma(xsrc(n, k), xT[n, :, k, :], [], f"d_xT{k}")
                return
            w = [T["xl", n, k - 2] if k >= 2 else T["xl", n - 1, k + 2 if n > 1 else k]]
            T["xT", n, k] = dma(xraw[:, k % 2, :], xT[n, :, k, :], w, f"d_xT{k % 2}")

        def nload(h):
            T["nl", h] = dma(rows[:, h % 8, :], w13[:, h, :], [T["nm", h - 8]] if h >= 8 else [], f"d_n{h % 8}")

        k_sm = dma(wsm[:, 0:NSM], small, [], "d_small")
        for q in range(4):
            load_xT(0, q)
        k_cst = dma(cs[:, :], cst, [], "d_cst")
        for q in (3, 0, 2, 1):
            if q == 1:
                for h in range(4):
                    nload(h)
            T["w2", q] = dma(F1[:, q * 2048:(q + 1) * 2048], w2[:, q * 2048:(q + 1) * 2048], [], f"d_w2{q}")
            if q == 0:
                load_x(0)
                k_tab = [dma(t[:, :], tab[i], [], f"d_tab{i}") for i, t in enumerate((cosT, sinT))]


        R = ring[:, 4:8, :].rearrange("p a b -> p (a b)")
        G, U = PG[:, :], PU[:, :]

        def small_c():
            m1, m2 = st[:, 0:1], st[:, 1:2]
            k1 = red(m1, wsm[:, WTK:WTK + 512], ALU.add, [k_sm])
            k2 = red(m2, wsm[:, WCT:WCT + 64], ALU.add, [k_sm])
            k1 = ts(m1, m1, 1.0 / 512, None, ALU.mult, None, [k1])
            k2 = ts(m2, m2, 1.0 / 64, None, ALU.mult, None, [k2])
            kt = ts(R[:, 0:512], wsm[:, WTK:WTK + 512], m1, None, ALU.subtract, None, [k1])
            kc = ts(R[:, 512:576], wsm[:, WCT:WCT + 64], m2, None, ALU.subtract, None, [k2])
            T["km"] = mm([(G[:, k * 64:(k + 1) * 64], R[:, k * 128:(k + 1) * 128], R[:, 512:576], True, True)
                          for k in range(4)], [kt, kc])

        def small_c2():
            km, xv = T["km"], G[:, 0:256].rearrange("p (k c) -> p k c", k=4)
            kh = act(Wc[:, :, 0:64], xv, ACT.Copy, [km])
            T["Wc"] = tt(Wc[:, :, 64:128], xv, Wc[:, :, 0:64].bitcast(F32), ALU.subtract, [kh])

        def small_i():
            return act(id16[:, :], idn, ACT.Copy, [k_cst])

        def small_p():
            wf = R[:, 576:832].rearrange("p (i c) -> p i c", i=2)
            wg = R[:, 832:1088].rearrange("p (i c) -> p i c", i=2)
            for i, base in enumerate((WQ, WK)):
                src = wsm[:, base:base + 64]
                ts(wf[:, i, 0:64], src, 1.0, None, ALU.mult, None, [k_sm])
                ts(wf[:, i, 64:96], src[:, 32:64], -1.0, None, ALU.mult, None, [k_sm])
                k = ts(wf[:, i, 96:128], src[:, 0:32], 1.0, None, ALU.mult, None, [k_sm])
            kb = mm([(U[:, i:i + 1], wf[0:64, i, :], bet[0:64, :], True, True) for i in range(2)], [k])
            T["pbias"] = P.put("vector", lambda e: e.tensor_copy(pbias[:, :], U[:, 0:2]), [kb], "dve")
            kg = ts(wg, wf, gam, None, ALU.mult, None, [k])
            kh = act(Wph[:, :, :], wg, ACT.Copy, [kg])
            T["Wp"] = tt(Wpl[:, :, :], wg, Wph[:, :, :].bitcast(F32), ALU.subtract, [kh])

        def small_m():
            T["ka"] = tt(R[:, 0:512], wsm[:, WTK:WTK + 512], wsm[:, WOR:WOR + 512], ALU.add, [k_sm, T["km"]])

        def small_m1():
            k1 = mm([(U[0:64, :], wsm[:, WCL:WCL + 64], R[:, 0:512], True, True)], [T["ka"], T["pbias"]])
            kt = act(R[0:64, 1088:1600], U[0:64, :], ACT.Copy, [k1, T["Wp"]])
            k2 = mm([(G, wsm[0:64, WV:WV + 128], R[0:64, 1088:1600], True, True)], [kt, T["Wc"]])
            kM = act(R[:, 0:512], G, ACT.Copy, [k2, k1])
            T["m2"] = kM, kt

        def small_m2():
            kM, kt = T["m2"]
            kb = mm([(U, bet[0:64, :].broadcast_to([64, 128]), R[0:64, 0:512], True, True)], [kM, kt])
            kg = ts(R[:, 576:1088], R[:, 0:512], gam, None, ALU.mult, None, [kM])
            kh = act(Mh[:, :], R[:, 576:1088], ACT.Copy, [kg])
            T["bb"] = tt(bb[:, :], U, wsm[:, BIAS:BIAS + 512], ALU.add, [kb])
            T["M2"] = act(Ml[64:128, :], R[64:128, 576:1088], ACT.Copy, [kg])
            T["M"] = tt(Ml[0:64, :], R[0:64, 576:1088], Mh[0:64, :].bitcast(F32), ALU.subtract, [kh])

        def parts_o(b, h, l, waits):
            k = P.put("vector", lambda e: e.tensor_copy(h[:, :], b), waits, "dve")
            T["o2"] = act(l[0:64, :], h[0:64, :].bitcast(F32), ACT.Copy, [k] + waits)
            T["o"] = tt(l[64:128, :], b[0:64, :], h[0:64, :].bitcast(F32), ALU.subtract, [k] + waits)

        def attention(n):
            c, first = n % 2, n == 0
            pos = c * 512

            def stats():
                if n:
                    load_x(n)

            def xstats(ts_):
                for t in ts_:
                    r = (n % 2) * 4 + t
                    k = P.put("vector", lambda e, t=t, r=r: e.bn_stats(st[:, 8 + 6 * t:14 + 6 * t], ring[:, r, :]),
                              [T["x", n, t]], "dve")
                    T["xs1", n, t] = k
                for t in ts_:
                    r = (n % 2) * 4 + t
                    k = P.put("vector", lambda e, t=t: e.bn_aggr(st[:, 32 + 2 * t:34 + 2 * t], st[:, 8 + 6 * t:14 + 6 * t]),
                              [T["xs1", n, t]], "dve")
                T["xst", n] = k
                if n:
                    bias(ts_)

            def bias(ts_):
                for t in ts_:
                    r = (n % 2) * 4 + t
                    T["xb", n, t] = tt(ring[:, r, :], ring[:, r, :], bb[:, :], ALU.add,
                                       [T["xs1", n, t], T["bb"]], "pool", "gpsimd")

            def xparts(k):
                return (Kh[:, 512:1024], Kl[:, 512:1024]) if first and k % 2 else (xh[:, :], xl[:, :])

            def conv(k):
                def go():
                    h, l = xparts(k)
                    free = T.get(("cp", n, k - 2)) if first else T["cp", n, k - 1] if k else T["cp", n - 1, 3]
                    T["xh", n, k] = act(h, xsrc(n, k), ACT.Copy, [T["xT", n, k], free])
                    T["xl", n, k] = tt(l, xsrc(n, k), h.bitcast(F32), ALU.subtract, [T["xh", n, k], free])
                    if n and k < 2:
                        load_xT(n, k + 2)
                return go

            def cproj(k):
                def go():
                    T["cp", n, k] = mm([(X, Wc[:, k, :], xparts(k)[0], k == 0, False),
                                        (X, Wc[:, k, :], xparts(k)[1], False, k == 3)],
                                       [T["xl", n, k], T["Wc"]] + ([T.pop("Xfree")] if k == 0 else []))
                return go

            def latent():
                T["cT"] = act(xTc[:, :], X, ACT.Copy, [T["cp", n, 3], T.get("xsfree")])
                T["Xfree"] = T["cT"]

            def latent2():
                T["ct"] = mm([(Y[:, t * 64:t * 64 + 64], xTc[:, t * 128:(t + 1) * 128], idd, True, True)
                              for t in range(4)], [T["cT"], T.pop("Yfree"), k_cst])
                c0 = PB[:, 0:256]
                T["c0"] = T["Yfree"] = act(c0, Y[:, 0:256], ACT.Copy, [T["ct"], T.get("PBfree"), T.get("Ph")])

            def squares():
                c0, c1 = PB[:, 0:256], PB[:, 256:512]
                k = tt(c1, c0, c0, ALU.mult, [T["c0"], T.get("PBfree")])
                T["sq"] = red(st[:, 40:44], c1.rearrange("p (t c) -> p t c", t=4), ALU.add, [k])

            def norm1():
                c0, c1 = PB[:, 0:256], PB[:, 256:512]
                c3 = c0.rearrange("p (t c) -> p t c", t=4)
                k = T["sq"]
                var = st[:, 32:40].rearrange("p (t c) -> p t c", t=4)[:, :, 1]
                k2 = ts(st[:, 44:48], var, EPS, EPS * EPS, ALU.mult, ALU.add, [T["xst", n]])
                k = stt(st[:, 48:52], st[:, 40:44], 1.0 / 64, st[:, 44:48], ALU.mult, ALU.add, [k, k2])
                k = rsqrt(st[:, 48:52], st[:, 52:56], st[:, 56:60], sti[:, 0:4], [k])
                k = ts(st[:, 52:56], st[:, 52:56], 256.0, None, ALU.mult, None, [k])
                cn = c1.rearrange("p (t c) -> p t c", t=4)
                k = tt(cn, c3, st[:, 52:56].unsqueeze(2).broadcast_to([128, 4, 64]), ALU.mult, [k])
                vh, vl = V[:, 4 * c:4 * c + 4, 0:64], V[:, 4 * c:4 * c + 4, 64:128]
                k = P.put("vector", lambda e: e.tensor_copy(vh, cn), [k, T.get("PVlast")], "dve")
                T["V", n] = tt(vl, cn, vh, ALU.subtract, [k])

            def vT():
                k = tr([(X16[:, t * 128:(t + 1) * 128], V[:, 4 * c + t, :]) for t in range(4)], id16[:, :],
                       [T["V", n], T.pop("Xfree"), k_i16])
                T["VT"] = act(VT[:, :], X16[:, 0:512], ACT.Copy, [k, T.get("VTfree")], scale=1.0 / 256)
                T["Xfree"] = T["VT"]

            def proj():
                T["pj"] = mm([(b, w[:, i, :], VT[:, :], z == 0, z == 1) for i, b in ((1, Y), (0, X))
                              for z, w in enumerate((Wph, Wpl))],
                             [T["VT"], T.pop("Xfree"), T.pop("Yfree"), T["Wp"]])
                T["VTfree"] = T["pj"]

            def rope(i):
                def go():
                    bank, name = ((X, "Xfree"), (Y, "Yfree"))[i]
                    a, b = (sil[0:64, :], hd[0:64, :]) if first and i else (PB[0:64, 0:512], PB[0:64, 512:1024])
                    w = [T["pj"], T["V", n], T.get("rope"), T.get("PBfree"), T["pbias"]]
                    ka = stt(a, bank[0:64, :], pbias[0:64, i:i + 1], cosT[0:64, pos:pos + 512], ALU.add, ALU.mult, w + [k_tab[0]])
                    kb = stt(b, bank[64:128, :], pbias[64:128, i:i + 1], sinT[64:128, pos:pos + 512], ALU.add, ALU.mult,
                             w + [k_tab[1]])
                    T[name] = kb
                    k = tt(a, a, b, ALU.add, [ka, kb])
                    if i == 0:
                        kq = act(Q[0:64, :], a, ACT.Copy, [k, T.get("Qfree")])
                        T["rope"] = T["Q"] = tt(Q[64:128, :], a, Q[0:64, :].bitcast(F32), ALU.subtract, [kq, T.get("Qfree")])
                    else:
                        h = Kh[0:64, pos:pos + 512]
                        kk = act(h, a, ACT.Copy, [k, T.get("Qfree")])
                        T["K2"] = act(Kh[64:128, pos:pos + 512], h.bitcast(F32), ACT.Copy, [kk, T.get("Qfree")])
                        T["rope"] = T["K"] = tt(Kl[0:64, pos:pos + 512], a, h.bitcast(F32), ALU.subtract, [kk, T.get("Qfree")])
                return go

            def tile(ti):
                t, ns = ti % 4, ti + 1
                W = max(256, ns * 128)
                r = (n % 2) * 4 + t
                q = Q[:, t * 128:(t + 1) * 128]
                c_ = 64 + 8 * (ti % 2)
                nmax, rsum, rinv = st[:, c_:c_ + 1], st[:, c_ + 1:c_ + 2], st[:, c_ + 2:c_ + 3]

                def scores():
                    parts = []
                    for a in range(0, W, 512):
                        z = min(W, a + 512)
                        if z - a < 256:
                            z = a + 256
                        parts += [(XY[:, a:z], q, Kh[:, a:z], True, False), (XY[:, a:z], q[0:64, :], Kl[0:64, a:z], False, True)]
                    w = [T["Q"], T["K"], T["K2"], T.pop("Xfree")] + ([T.pop("Yfree")] if W > 512 else [])
                    k = mm(parts, w)
                    T["Qfree"] = k
                    d = (ns - 1) * 128
                    k = tt(XY[:, d:d + 128], XY[:, d:d + 128], msk[:, 0:128], ALU.add, [k])
                    k = red(rsum, XY[:, 0:ns * 128], ALU.max, [k, T.get(("rinv", ti % 2))])
                    T["nmax"] = ts(nmax, rsum, -0.125, None, ALU.mult, None, [k, T.get(("exp", ti % 2))])

                def exps():
                    w = ns * 128
                    k = P.put("scalar", lambda e: e.activation(PB[:, 0:w], XY[:, 0:w], ACT.Exp, bias=nmax, scale=0.125,
                                                               accum_out=rsum), [T["nmax"], T.get("Pl"), T["rope"]], "act")
                    T["exp", ti % 2] = k
                    T["Xfree"] = k
                    if w > 512:
                        T["Yfree"] = k
                    for a in range(0, w, 512):
                        z = min(w, a + 512)
                        T["Ph", a] = T["Ph"] = act(Ph[:, a:z], PB[:, a:z], ACT.Copy, [k, T.get("Tlast")], scale=4096.0)

                def low():
                    w = ns * 128
                    for a in range(0, w, 512):
                        z = min(w, a + 512)
                        T["Pl", a] = T["Pl"] = stt(Pl[:, a:z], PB[:, a:z], 4096.0, Ph[:, a:z], ALU.mult, ALU.subtract,
                                                   [T["Ph", a], T.get("Tlast")])
                    T["PBfree"] = T["Pl"]
                    k = ts(rinv, rsum, float(2 ** 20), None, ALU.mult, None, [T["exp", ti % 2], T.get(("x2", ti % 2))])
                    T["rinv", ti % 2] = P.put("vector", lambda e: e.reciprocal(rinv, rinv), [k], "dve")

                def trans(g):
                    s0, s1 = 4 * g, min(ns, 4 * g + 4)
                    m = s1 - s0
                    k = tr([(Y16[:, (h * m + s) * 128:(h * m + s + 1) * 128], (Ph, Pl)[h][:, (s0 + s) * 128:(s0 + s + 1) * 128])
                            for h in range(2) for s in range(m)], id16[:, :], [T["Pl", 512 * g], T.pop("Yfree")])
                    T["Tlast"] = k
                    k = act(PT[:, g, 0:2 * m * 128], Y16[:, 0:2 * m * 128], ACT.Copy, [k, T.get(("PVg", g))])
                    T["Yfree"] = T["PT", g] = k

                def pv(g):
                    s0, s1 = 4 * g, min(ns, 4 * g + 4)
                    m = s1 - s0
                    parts = [(X[:, 0:128], V[:, s0 + s, :], PT[:, g, (h * m + s) * 128:(h * m + s + 1) * 128],
                              s0 + s == 0 and h == 0, s0 + s == ns - 1 and h == 1)
                             for s in range(m) for h in range(2)]
                    k = mm(parts, [T["PT", g]] + ([T.pop("Xfree")] if g == 0 else []))
                    T["PVg", g] = T["PVlast"] = k
                    if s1 == ns:
                        parts_o(X[:, 0:128], oh, ol, [k, T.get("opm")])
                        T["Xfree"] = T["o"]

                def outp():
                    T["opm"] = k = mm([(Y, oh[:, :], Mh[:, :], True, False), (Y, ol[:, :], Ml[:, :], False, True)],
                                      [T["o"], T["o2"], T.pop("Yfree"), T["M"], T["M2"]])
                    xt = ring[:, r, :]
                    k = stt(xt, Y, rinv, xt, ALU.mult, ALU.add, [k, T["rinv", ti % 2], T["xb", n, t]])
                    T["x2", ti % 2] = T["Yfree"] = k
                    k = P.put("vector", lambda e: e.bn_stats(st[:, 80:86], xt), [k], "dve")
                    k = P.put("vector", lambda e: e.bn_aggr(st[:, 86:88], st[:, 80:86]), [k], "dve")
                    k = ts(st[:, 88:89], st[:, 87:88], EPS, None, ALU.add, None, [k])
                    k = rsqrt(st[:, 88:89], st[:, 89:90], st[:, 90:91], sti[:, 8:9], [k])
                    k = ts(st[:, 89:90], st[:, 89:90], 1024.0, None, ALU.mult, None, [k])
                    k = ts(xs[:, :], xt, st[:, 86:87], st[:, 89:90], ALU.subtract, ALU.mult, [k, T.get("xh16"), T["ct"]])
                    T["xh16"] = act(xnp[:, 0, :], xs[:, :], ACT.Copy, [k, T.get("XT")])
                    T["xn16"] = tt(xnp[:, 1, :], xs[:, :], xnp[:, 0, :], ALU.subtract, [T["xh16"], T.get("XT")])
                    T["xsfree"] = T["xn16"]

                def xtr():
                    T["XT"] = k = tr([(X16[:, (h * 4 + j) * 128:(h * 4 + j + 1) * 128], xnp[:, h, j * 128:(j + 1) * 128])
                                      for h in range(2) for j in range(4)], id16[:, :], [T["xn16"], T.pop("Xfree")])
                    k = act(xnT[n % 2][:, :, :, t * 128:(t + 1) * 128], X16.rearrange("p (h j c) -> p h j c", h=2, j=4),
                            ACT.Copy, [k, T.get(("Uend", n - 2))])
                    T["Xfree"] = T["xn", n, t] = k

                b = 15 + 7 * t
                plan = [(b, scores), (b + 1, exps), (b + 2, low), (b + 3, lambda: trans(0)), (b + 4, lambda: pv(0)),
                        (b + 6, outp), (b + 10 - (t == 3), xtr)]
                if ns > 4:
                    plan += [(b + 4, lambda: trans(1)), (b + 5, lambda: pv(1))]
                return plan

            if first:
                front = {f"conv{k}": conv(k) for k in range(4)} | {f"cproj{k}": cproj(k) for k in range(4)}
                return front | {"latent": latent, "latent2": latent2, "xstats": xstats, "bias": bias, "squares": squares, "norm1": norm1,
                                "vT": vT, "proj": proj, "ropeK": rope(1), "ropeQ": rope(0)}
            plan = [(0, conv(0)), (3, stats), (5, latent), (5, latent2), (6, squares), (6, lambda: xstats((0, 1))),
                    (7, lambda: xstats((2, 3))), (8, norm1), (11, vT), (12, proj), (12, rope(1)), (13, rope(0))]
            for k in range(4):
                plan.append((k + 1, cproj(k)))
                if k < 3:
                    plan.append((k + 1, conv(k + 1)))
            for ti in range(4 * c, 4 * c + 4):
                plan += tile(ti)
            return sorted(plan, key=lambda s: s[0])

        s16 = sil[:, :].bitcast(F16)
        span = [slice(0, 128), slice(128, 384), slice(384, 768)]
        E0 = [PB[:, s] for s in span] + [hd[:, :]]
        H0 = [Ph[:, s] for s in span] + [s16[:, 0:512]]
        L0 = [Pl[:, s] for s in span] + [s16[:, 512:1024]]

        def col0(t, i):
            return st[:, 64 + 4 * t + i:65 + 4 * t + i]

        def scores0(t):
            W, s = max(256, t * 128 + 128), PD[:, t, :]
            q = Q[:, t * 128:(t + 1) * 128]
            T["Qfree"] = k = mm([(s[:, 0:W], q, Kh[:, 0:W], True, False), (s[:, 0:W], q[0:64, :], Kl[0:64, 0:W], False, True)],
                                [T["Q"], T["K"], T["K2"]])
            d = s[:, t * 128:(t + 1) * 128]
            T["sc0", t] = tt(d, d, msk[:, 0:128], ALU.add, [k])

        def max0(t):
            k = red(col0(t, 1), PD[:, t, 0:t * 128 + 128], ALU.max, [T["sc0", t]])
            T["max0", t] = ts(col0(t, 0), col0(t, 1), -0.125, None, ALU.mult, None, [k])

        def exp0(t):
            w = t * 128 + 128
            T["exp0", t] = P.put("scalar", lambda e: e.activation(
                E0[t], PD[:, t, 0:w], ACT.Exp, bias=col0(t, 0), scale=0.125, accum_out=col0(t, 1)), [T["max0", t], T["rope"]], "act")

        def high0(t):
            T["Ph0", t] = act(H0[t], E0[t], ACT.Copy, [T["exp0", t]], scale=4096.0)

        def low0(t):
            T["Pl0", t] = T["PBfree"] = T["Pl"] = stt(L0[t], E0[t], 4096.0, H0[t], ALU.mult, ALU.subtract, [T["Ph0", t]])
            k = ts(col0(t, 2), col0(t, 1), float(2 ** 20), None, ALU.mult, None, [T["exp0", t]])
            T["rinv0", t] = P.put("vector", lambda e: e.reciprocal(col0(t, 2), col0(t, 2)), [k], "dve")

        def trans0(t):
            m, g, name = t + 1, t % 2, "XY"[t % 2] + "free"
            b = (X16, Y16)[t % 2]
            T["Tlast"] = T["tr0", t] = k = tr([(b[:, (h * m + s) * 128:(h * m + s + 1) * 128], (H0, L0)[h][t][:, s * 128:(s + 1) * 128])
                                               for h in range(2) for s in range(m)], id16[:, :], [T["Pl0", t], T.pop(name)])
            T["PT0", t] = T[name] = act(PT[:, g, 0:2 * m * 128], b[:, 0:2 * m * 128], ACT.Copy, [k, T.get(("PVg", g))])

        O0 = ((oh[:, :], ol[:, :]), (VT[:, 0:128], VT[:, 128:256]))

        def pv0(t):
            m, g, b = t + 1, t % 2, PD[:, t, 0:128]
            h, l = O0[g]
            parts = [(b, V[:, s, :], PT[:, g, (h * m + s) * 128:(h * m + s + 1) * 128], (s, h) == (0, 0), (s, h) == (m - 1, 1))
                     for s in range(m) for h in range(2)]
            T["PVg", g] = T["PVlast"] = k = mm(parts, [T["PT0", t], T["exp0", t]])
            parts_o(b, h, l, [k, T.get(("op0", t - 2)), T["VTfree"]])
            T["o", t], T["o2", t] = T["o"], T["o2"]

        def outp0(t):
            b, xt = PD[:, t, :], ring[:, t, :]
            h, l = O0[t % 2]
            T["opm"] = T["op0", t] = k = mm([(b, h, Mh[:, :], True, False), (b, l, Ml[:, :], False, True)],
                                            [T["o", t], T["o2", t], T["M"], T["M2"]])
            k = stt(xt, b, col0(t, 2), xt, ALU.mult, ALU.add, [k, T["rinv0", t], T["xb", 0, t]])
            T["x2", t % 2] = k
            T["bn0", t] = P.put("vector", lambda e: e.bn_stats(st[:, 8 + 6 * t:14 + 6 * t], xt), [k], "dve")

        def norm0():
            for t in range(4):
                k = P.put("vector", lambda e, t=t: e.bn_aggr(st[:, 32 + 2 * t:34 + 2 * t], st[:, 8 + 6 * t:14 + 6 * t]),
                          [T["bn0", t]], "dve")
            var = st[:, 32:40].rearrange("p (t c) -> p t c", t=4)[:, :, 1]
            k = ts(st[:, 80:84], var, EPS, None, ALU.add, None, [k])
            k = rsqrt(st[:, 80:84], st[:, 84:88], st[:, 88:92], sti[:, 4:8], [k])
            T["rs0"] = ts(st[:, 84:88], st[:, 84:88], 1024.0, None, ALU.mult, None, [k])

        def xnorm0(t):
            g = t % 2
            f = (xs, hd)[g][:, :]
            p = (xnp[:, :, :], s16.rearrange("p (h c) -> p h c", h=2))[g]
            k = ts(f, ring[:, t, :], st[:, 32 + 2 * t:33 + 2 * t], st[:, 84 + t:85 + t], ALU.subtract, ALU.mult,
                   [T["rs0"], T["xn0", t - 2] if t > 1 else T["ct"]])
            free = T["XT0", t - 2] if t > 1 else T["tr0", 3]
            k = T["xh16"] = act(p[:, 0, :], f, ACT.Copy, [k, free])
            T["xn0", t] = T["xsfree"] = tt(p[:, 1, :], f, p[:, 0, :], ALU.subtract, [k, free])

        def xtr0(t):
            g, name = t % 2, "XY"[t % 2] + "free"
            b = (X16, Y16)[g]
            p = (xnp[:, :, :], s16.rearrange("p (h c) -> p h c", h=2))[g]
            T["XT"] = T["XT0", t] = k = tr([(b[:, (h * 4 + j) * 128:(h * 4 + j + 1) * 128], p[:, h, j * 128:(j + 1) * 128])
                                            for h in range(2) for j in range(4)], id16[:, :], [T["xn0", t], T.pop(name)])
            o, i = xnT[0][:, :, :, t * 128:(t + 1) * 128], b.rearrange("p (h j c) -> p h j c", h=2, j=4)
            if g:
                k = P.put("vector", lambda e: e.tensor_copy(o, i), [k], "dve")
            else:
                k = act(o, i, ACT.Copy, [k])
            T[name] = T["xn", 0, t] = k

        def butterfly(q, s, op):
            eng, sem = ("gpsimd", "pool") if q > 1 else ("vector", "dve")
            a, b = F1[:, q * 2048:(q + 1) * 2048], F0[:, q * 2048:(q + 1) * 2048]
            src, dst = ((a, b), (b, a))[s]
            pat = "p (g two n) -> p two g n" if s == 0 else "p (two g n) -> p two g n"
            u, v = src.rearrange(pat, two=2, n=512), dst.rearrange(pat, two=2, n=512)
            w = [T["w2", q]] if s == 0 else [T["bf", q, 0, 0], T["bf", q, 0, 1]]
            T["bf", q, s, op] = tt(v[:, op], u[:, 0], u[:, 1], (ALU.add, ALU.subtract)[op], w, sem, eng)

        def butterfly3(g, half, op):
            eng, sem = ("gpsimd", "pool") if g else ("vector", "dve")
            o = g * 4096 + half * 1024
            w = [T["bf", 2 * g + i, 1, j] for i in range(2) for j in range(2)]
            T["b3", g, half, op] = tt(F0[:, o + 2048 * op:o + 2048 * op + 1024], F1[:, o:o + 1024], F1[:, o + 2048:o + 3072],
                                      (ALU.add, ALU.subtract)[op], w, sem, eng)

        def butterfly4(i, op):
            eng, sem = ("gpsimd", "pool") if i < 3 else ("vector", "dve")
            o = i * 1024
            w = [T["b3", g, i % 2, i // 2] for g in range(2)] + [T["b3", op, i % 2, j] for j in range(2)]
            T["b4", i, op] = tt(F1[:, o + 4096 * op:o + 4096 * op + 1024], F0[:, o:o + 1024], F0[:, o + 4096:o + 5120],
                                (ALU.add, ALU.subtract)[op], w, sem, eng)

        def norms(h):
            for w in range(2):
                junk = hT[:, h % 2, w, :].bitcast(BF16)
                c = 96 + w * 16 + h
                T["nm", h] = P.put("scalar", lambda e, w=w, junk=junk, c=c: e.activation(
                    junk, rows[:, h % 8, w * 512:(w + 1) * 512], ACT.Square, accum_out=st[:, c:c + 1]),
                    [T["nl", h], T.get(("nm", h - 2))], "act")
            if h < 8:
                nload(h + 8)

        def scales():
            n2, e = st[:, 96:128], sti[:, 16:48]
            k = ts(n2, n2, 1e-30, 1e30, ALU.max, ALU.min, [T["nm", NH - 1]])
            k = ts(e, n2.bitcast(I32), 23, None, ALU.logical_shift_right, None, [k])
            k = ts(e, e, 1.0, None, ALU.add, None, [k])
            ke = ts(e, e, 1, None, ALU.logical_shift_right, None, [k])

            T["sc1"] = power(st[:, 128:160], e, -1.0, 204.0, [ke])

        def power(dst, src, mul, add, waits):
            s = sti[:, 48:48 + src.shape[1]]
            k = ts(s, src, mul, add, ALU.mult, ALU.add, waits)
            return ts(dst.bitcast(I32), s, 23, None, ALU.logical_shift_left, None, [k])

        def scales1():
            e, k = sti[:, 16:48], T["sc1"]
            k = power(afs[:, 0:16], e[:, 0:16], 1.0, 40.0, [k])
            k = power(afs[:, 16:32], e[:, 0:16], -1.0, 172.0, [k])
            k = tt(e[:, 0:16], e[:, 0:16], e[:, 16:32], ALU.add, [k])
            k = power(afs[:, 32:48], e[:, 0:16], 1.0, -5.0, [k])
            T["sc"] = ts(afs[:, 32:48], afs[:, 32:48], float(np.float32(1.0 / np.sqrt(2048))), None, ALU.mult, None, [k])

        def fwht(j):
            b = (PG, PU)[j % 2]
            T["fm", j] = k = mm([(b[:, :], had, F1[:, j * 512:(j + 1) * 512], True, True)],
                                [T["b4", j % 8 // 2, j // 8], T.get(("bank", j % 2)), T["bb"], T["M"]])
            T["fe", j] = T["bank", j % 2] = act(F1[:, j * 512:(j + 1) * 512], b[:, :], ACT.Copy, [k])

        def stat2(j):
            if j % 2:
                junk = hT[:, 0, j // 2 % 2, :].bitcast(BF16)
                T["mxa", j // 2 % 2] = T["mxa"] = P.put("scalar", lambda e: e.activation(
                    junk, F1[:, j * 512:(j + 1) * 512], ACT.Square, accum_out=afs[:, 48 + j:49 + j]),
                    [T["fe", j], T["nm", NH - 1], T.get(("mxa", j // 2 % 2))], "act")
                return
            k = P.put("vector", lambda e: e.bn_stats(bn2[:, j, :], F1[:, j * 512:(j + 1) * 512]), [T["fe", j]], "dve")
            T["mx"] = P.put("vector", lambda e: e.bn_aggr(mv2[:, j, :], bn2[:, j, :]), [k], "dve")

        def scale2():
            g, e_ = st[:, 4:5], sti[:, 12:13]
            m, v = (mv2[:, :, i].rearrange("p (j two) -> p two j", two=2)[:, 0] for i in range(2))
            q = afs[:, 48:64].rearrange("p (j two) -> p two j", two=2)[:, 0]
            k = tt(q, m, m, ALU.mult, [T["mx"]])
            k = tt(q, q, v, ALU.add, [k])
            k = ts(q, q, 512.0, None, ALU.mult, None, [k])
            k = tt(afs[:, 48:64], afs[:, 48:64], afs[:, 32:48], ALU.mult, [k, T["sc"], T["mxa"]])
            k = tt(afs[:, 48:64], afs[:, 48:64], afs[:, 32:48], ALU.mult, [k])
            k = red(g, afs[:, 48:64], ALU.max, [k])
            k = P.put("gpsimd", lambda e: e.partition_all_reduce(st[:, 5:6], g, 128, bass.bass_isa.ReduceOp.max), [k], "pool")
            k = ts(st[:, 5:6], st[:, 5:6], 1e-30, 1e30, ALU.max, ALU.min, [k])
            k = ts(e_, st[:, 5:6].bitcast(I32), 23, None, ALU.logical_shift_right, None, [k])
            k = ts(e_, e_, 1.0, None, ALU.add, None, [k])
            k = ts(e_, e_, 1, None, ALU.logical_shift_right, None, [k])
            k = ts(sti[:, 13:14], e_, -1.0, 205.0, ALU.mult, ALU.add, [k])
            k = ts(afs[:, 64:65].bitcast(I32), sti[:, 13:14], 23, None, ALU.logical_shift_left, None, [k])
            k = ts(sti[:, 14:15], e_, 1.0, 49.0, ALU.mult, ALU.add, [k])
            ts(afs[:, 65:66].bitcast(I32), sti[:, 14:15], 23, None, ALU.logical_shift_left, None, [k])
            T["s2"] = ts(afs[:, 32:48], afs[:, 32:48], afs[:, 64:65], None, ALU.mult, None, [k])

        def split2(j):
            f = F1[:, j * 512:(j + 1) * 512]
            k = act(W2[:, j, 0, :], f, ACT.Copy, [T["s2"]], scale=afs[:, 32 + j:33 + j])
            if j < 2:
                T["W2", j] = stt(W2[:, j, 1, :], f, afs[:, 32 + j:33 + j], W2[:, j, 0, :], ALU.mult, ALU.subtract, [k])
                return
            k = pool_ts(f, f, afs[:, 32 + j:33 + j], ALU.mult, [k])
            T["W2", j] = tt(W2[:, j, 1, :], f, W2[:, j, 0, :], ALU.subtract, [k], "pool", "gpsimd")

        def wload(u):
            T["wl", u] = dma(raw[:, u % 2, :], w13[:, u // 2, u % 2 * 512:u % 2 * 512 + 512],
                             [T["wn", u - 2]] if u >= 2 else [], f"d_w{u % 2}")

        def wsplit(u):
            c = 128 + u % 2 * 16 + u // 2
            r, h, l, s1 = raw[:, u % 2, :], wn[:, u % 2, 0, :], wn[:, u % 2, 1, :], st[:, c:c + 1]
            k = act(h, r, ACT.Copy, [T["wl", u], T["sc1"], T.get(("wt", u - 2))], scale=s1)
            T["wn", u] = stt(l, r, s1, h, ALU.mult, ALU.subtract, [k, T.get(("wt", u - 2))])
            if u < 2 * NH - 2:
                wload(u + 2)

        def wtrans(u, eng=0):
            h = u // 2
            free = [T["b4", i, op] for i in range(4) for op in range(2)] if h < 8 else [T["W2", 2 * h - 15]]
            T["wt", u] = k = tr([(Y16[:, (i * 4 + j) * 128:(i * 4 + j + 1) * 128], wn[:, u % 2, i, j * 128:(j + 1) * 128])
                                 for i in range(2) for j in range(4)], id16[:, :], [T["wn", u], T.pop("Yfree"), k_i16])
            d = WA[:, u * 1024:(u + 1) * 1024]
            if eng:
                k = act(d, Y16, ACT.Copy, [k] + free)
            else:
                k = P.put("vector", lambda e: e.tensor_copy(d, Y16), [k] + free, "dve")
            T["Yfree"] = T["wp", u] = k

        def product(bank, n, h, w, waits, sem):
            base = h * 2048 + w * 1024
            parts = []
            for k in range(4):
                wh = WA[:, base + k * 128:base + (k + 1) * 128]
                wl = WA[:, base + 512 + k * 128:base + 512 + (k + 1) * 128]
                xa, xb_ = xnT[n % 2][:, 0, k, :], xnT[n % 2][:, 1, k, :]
                parts += [(bank[:, :], wh, xa, k == 0, False), (bank[:, :], wh, xb_, False, False),
                          (bank[:, :], wl, xa, False, k == 3)]
            return mm(parts, waits, sem)

        def gate(n, h):
            w = [T["xn", n, t] for t in range(4)] + ([T["wp", 2 * h]] if n == 0 else [])
            T["G"] = product(PG, n, h, 0, w + [T.get("silu"), T["bank", 0]], "g")

        def silu(h):
            T["silu"] = act(sil[:, :], PG[:, :], ACT.Silu, [T["G"], T.get("hd")], "silu", scale=afs[:, h:h + 1])

        def up(n, h):
            b = h % 2
            T["U"] = product(PU, n, h, 1, [T.get("hd"), T["bank", 1]] + ([T["wp", 2 * h + 1]] if n == 0 else []), "u")
            if h == NH - 1:
                T["Uend", n] = T["U"]
            T["hd"] = stt(hd[:, :], PU[:, :], afs[:, 16 + h:17 + h], sil[:, :], ALU.mult, ALU.mult,
                          [T["U"], T["silu"], T.get("hi"), T.get(("lo", 1 - b))], "hd")

        def halves(h):
            b = h % 2
            T["hi"] = act(hT[:, b, 0, :], hd[:, :], ACT.Copy, [T["hd"], T.get(("D", b))], "hi")
            T["lo", b] = tt(hT[:, b, 1, :], hd[:, :], hT[:, b, 0, :], ALU.subtract, [T["hi"], T.get(("D", b))], "lo")

        def down(n, h):
            b = h % 2
            parts = []
            for t in range(4):
                a, z = hT[:, b, 0, t * 128:(t + 1) * 128], hT[:, b, 1, t * 128:(t + 1) * 128]
                parts += [(PD[:, t, :], a, W2[:, h, 0, :], h == 0, False), (PD[:, t, :], a, W2[:, h, 1, :], False, False),
                          (PD[:, t, :], z, W2[:, h, 0, :], False, h == NH - 1)]
            w = [T["lo", b]] + ([T["W2", h]] if n == 0 else []) + ([T["ev", n - 1]] if n and h == 0 else [])
            T["D", b] = mm(parts, w, "d")

        def finish(n):
            for t in range(4):
                r = (n % 2) * 4 + t
                T["ev", n] = stt(ring[:, r, :], PD[:, t, :], afs[:, 65:66], ring[:, r, :], ALU.mult, ALU.add,
                                 [T["D", (NH - 1) % 2]], "ev")
                T["store", n, t] = dma(out[(n * 4 + t) * 128:(n * 4 + t + 1) * 128, :], ring[:, r, :], [T["ev", n]], f"d_o{r}")

        A = attention(0)
        low = [lambda a=(q, s, op): butterfly(*a) for q in (0, 1) for s in range(2) for op in range(2)]
        low += [lambda a=(0, i, op): butterfly3(*a) for i in range(2) for op in range(2)]
        sq = [lambda h=h: norms(h) for h in range(NH)]
        fj = (0, 1, 8, 9, 2, 3, 10, 11, 4, 5, 12, 13, 6, 7, 14, 15)
        fw, s2 = [lambda j=j: fwht(j) for j in fj], [lambda j=j: stat2(j) for j in fj]

        def some(jobs, count):
            for _ in range(min(count, len(jobs))):
                jobs.pop(0)()

        for h in range(4, 8):
            nload(h)
        for h in range(2):
            wload(h)
        for q in (3, 2):
            for s_ in range(2):
                for op in range(2):
                    butterfly(q, s_, op)
        small_c()
        A["conv0"]()
        small_c2()
        A["conv1"]()
        A["cproj0"]()
        A["conv2"]()
        A["cproj1"]()
        A["conv3"]()
        A["cproj2"]()
        A["cproj3"]()
        k_i16 = small_i()
        A["latent"]()
        A["latent2"]()
        small_p()
        A["xstats"](range(4))
        A["squares"]()
        A["norm1"]()
        some(sq, 1)
        small_m()
        A["vT"]()
        some(sq, 2)
        some(low, 3)
        A["proj"]()
        A["ropeK"]()
        A["ropeQ"]()
        some(sq, 1)
        small_m1()
        some(sq, 3)
        some(low, 2)
        for i in range(2):
            for op in range(2):
                butterfly3(1, i, op)
        for t in range(4):
            scores0(t)
            max0(t)
        small_m2()
        A["bias"](range(4))
        some(low, 1)
        exp0(0)
        exp0(1)
        high0(0)
        exp0(2)
        high0(1)
        exp0(3)
        high0(2)
        high0(3)
        some(low, 2)
        low0(0)
        low0(1)
        some(low, 2)
        low0(2)
        low0(3)
        some(low, 2)
        for i in range(3):
            for op in range(2):
                butterfly4(i, op)
        for t in range(6):
            if t < 4:
                trans0(t)
            if 0 < t < 5:
                pv0(t - 1)
            if t > 1:
                outp0(t - 2)
            some(sq, 4 if t < 2 else 2)
            if t in (1, 2):
                butterfly4(3, t - 1)
            if t > 1:
                some(fw, 1 + t // 3)
            if t == 3:
                scales()
            if t == 4:
                scales1()
        norm0()
        some(fw, 5)
        xnorm0(0)
        xnorm0(1)
        some(s2, 2)
        wsplit(0)
        for t in range(4):
            xtr0(t)
            if t < 2:
                xnorm0(t + 2)
            some(fw, 1)
            some(s2, 2)
            if not t:
                wsplit(1)
        some(fw, 9)
        wtrans(0)
        wtrans(1, 1)
        wsplit(2)
        some(s2, 2)
        wsplit(3)
        some(s2, 1)
        assert not low + sq + fw
        load_xT(1, 0)
        load_xT(1, 1)

        for n in range(NC):
            plan = attention(n + 1) if n + 1 < NC else []
            if n + 2 < NC:
                plan.append((40, lambda: (load_xT(n + 2, 0), load_xT(n + 2, 1))))
            if n == 0:
                early, late = [], [(0, lambda: some(s2, 3)), (1, lambda: some(s2, 9)), (2, lambda: (scale2(), split2(0)))]
                for j in range(1, NH):
                    late.append((int(2.6 * j) + (j < 3), lambda j=j: split2(j)))
                at = (1, 2, 4, 5, 7, 8, 10, 11, 12, 13, 14, 17, 18, 19, 20, 21, 24, 25, 26, 27, 28, 31, 32, 33, 34, 35,
                      38, 40, 41, 42)
                for u, z in enumerate(at, 2):
                    early.append((z, lambda u=u, i=u % 2 and z not in (17, 24, 31, 38): wtrans(u, i)))
                    if u < 2 * NH - 2:
                        late.append((z, lambda u=u: wsplit(u + 2)))
                plan = [(s_ + 0.1 * i, f) for i, part in enumerate((early, plan, late)) for s_, f in part]
            plan.sort(key=lambda s: s[0])
            slot = 0

            def fill():
                nonlocal slot
                while plan and plan[0][0] < slot + 1:
                    plan.pop(0)[1]()
                slot += 1
            for h in range(NH):
                gate(n, h)
                silu(h)
                fill()
                up(n, h)
                fill()
                halves(h)
                if h:
                    down(n, h - 1)
                elif n:
                    down(n - 1, NH - 1)
                    finish(n - 1)
                if h < NH - 1:
                    fill()
            assert not plan
        down(NC - 1, NH - 1)
        finish(NC - 1)

        ends = [T["store", n, t] for n in (NC - 2, NC - 1) for t in range(4)]
        block = ctx.enter_context(nc.Block())

        @block.sync
        def _(eng):
            P.play("sync", eng)
            for s, v in ends:
                eng.wait_ge(P.sems[s], v)

        @block.tensor
        def _(eng):
            P.play("tensor", eng)

        @block.vector
        def _(eng):
            P.play("vector", eng)

        @block.scalar
        def _(eng):
            P.play("scalar", eng)

        @block.gpsimd
        def _(eng):
            P.play("gpsimd", eng)


def constants():
    i = np.arange(128)
    bits = np.array([bin(v).count("1") for v in range(128)])
    had = np.where(bits[i[:, None] & i[None, :]] % 2, -1.0, 1.0)
    two = np.concatenate([np.eye(64), np.eye(64)], 0)
    mask = np.where(np.arange(256)[None, :] <= i[:, None], 0.0, -1e30)
    cst = np.concatenate([had, np.eye(128), two, mask], 1).astype(np.float32)
    inv = np.float32(1) / (10000.0 ** (np.arange(0, 64, 2) / 64)).astype(np.float32)
    ang = (np.arange(1024, dtype=np.float32)[:, None] * inv[None, :]).T.astype(np.float64)
    ang = np.concatenate([ang] * 4, 0)
    return cst, np.stack([np.cos(ang), np.sin(ang)]).astype(np.float32)


def kernel(L0_attn_x, L0_attn_W_to_kv, L0_attn_W_compress, L0_attn_ln_gamma, L0_attn_ln_beta, L0_attn_W_q_comp,
           L0_attn_W_kv_comp, L0_attn_W_comp2lat, L0_attn_W_out_res, L0_attn_b_out_res, L0_ffn_W1, L0_ffn_W2, L0_ffn_W3):
    import concourse.bacc as bacc
    from concourse.bass_utils import run_bass_kernel_spmd

    a = np.asarray
    x = a(L0_attn_x).reshape(NC * 512, 512)
    xT = x.reshape(NC, 512, 4, 128).transpose(0, 3, 2, 1)
    w13 = np.stack([a(w).reshape(NH, 128, 512).transpose(1, 0, 2) for w in (L0_ffn_W1, L0_ffn_W3)], 2)
    w13 = w13.reshape(128, NH, 1024)
    w2 = a(L0_ffn_W2).T.reshape(NH, 128, 512).transpose(1, 0, 2).reshape(128, NH * 512)
    twice = lambda m: np.concatenate([m, m], 0)
    kv = a(L0_attn_W_kv_comp)
    wv = kv[64:128]
    col = lambda v: twice(a(v)[:, None])
    small = np.concatenate([
        a(L0_attn_W_to_kv), a(L0_attn_W_compress).T, twice(a(L0_attn_W_q_comp).T), twice(kv[0:64].T),
        twice(np.concatenate([wv, wv], 1)), a(L0_attn_W_comp2lat), a(L0_attn_W_out_res).T,
        col(L0_attn_ln_gamma), col(L0_attn_ln_beta), np.broadcast_to(a(L0_attn_b_out_res)[None, :], (128, 512))], 1)
    cst, tab = constants()
    arrays = {"x": x, "xT": xT, "w13": w13, "w2": w2, "small": small, "cst": cst, "tab": tab}
    arrays = {k: np.ascontiguousarray(v) for k, v in arrays.items()}
    nc = bacc.Bacc("TRN2", target_bir_lowering=False, num_devices=1)
    aps = {k: nc.dram_tensor(k, v.shape, mybir.dt.from_np(v.dtype), kind="ExternalInput").ap() for k, v in arrays.items()}
    out = nc.dram_tensor("out", (NC * 512, 512), F32, kind="ExternalOutput").ap()
    build_kernel(nc, out=out, **aps)
    r = run_bass_kernel_spmd(nc, [arrays], core_ids=[0])
    return r.results[0]["out"].reshape(8, 1024, 512)
```
